# Optimizing a Trainium2 kernel written in Bass

```python
import numpy as np
import jax
import jax.numpy as jnp

def _softmax(x, axis=-1):
    return jax.nn.softmax(x, axis=axis)

def _gelu(x):
    return jax.nn.gelu(x, approximate=True)

def _silu(x):
    return jax.nn.silu(x)

def _sigmoid(x):
    return jax.nn.sigmoid(x)

def _layernorm(x, axis=-1, eps=1e-05):
    m = jnp.mean(x, axis=axis, keepdims=True)
    v = jnp.var(x, axis=axis, keepdims=True)
    return (x - m) / jnp.sqrt(v + eps)

def _scatter_add(tgt, idx, src, axis=0):
    return tgt.at[idx].add(src)

def _segment_sum(src, seg, n):
    return jax.ops.segment_sum(src, seg, n)
kernel_name = 'mk_cond_seq_d2_seqx_r2_886ad0'

def setup_inputs(seed: int=0):
    np.random.seed(seed)
    _w = jnp.asarray

    def _rec_inputs():
        import jax
        import jax.numpy as jnp
        _rk = jax.random.key(seed)
        x = -0.0003929 + 0.9999 * jax.random.normal(jax.random.fold_in(_rk, 1), (8, 512, 512), jnp.float32)
        _lenS = 512 - jax.random.randint(jax.random.fold_in(_rk, 7), (8,), 0, max(1, 512 // 4) + 1, jnp.int32)
        _lenS2 = 512 - jax.random.randint(jax.random.fold_in(_rk, 8), (8,), 0, max(1, 512 // 4) + 1, jnp.int32)
        cond_2048 = 0.00782532 + 1.00527 * jax.random.normal(jax.random.fold_in(_rk, 11), (8, 1024), jnp.float32)
        _validS = jnp.arange(512)[None, :] < _lenS[:, None]
        _validS2 = jnp.arange(512)[None, :] < _lenS2[:, None]
        _causal = jnp.tril(jnp.ones((512, 512), dtype=bool))
        mask_BxS_ik0 = jnp.where(jnp.broadcast_to(_validS[:, :], (8, 512)), 0, 1).astype(jnp.int32)
        mask_BxSx1_fk1 = jnp.where(jnp.ones((8, 512, 1), dtype=bool), 1.0, 0.0).astype(jnp.float32)
        return (x, cond_2048, mask_BxS_ik0, mask_BxSx1_fk1)
    x, cond_2048, mask_BxS_ik0, mask_BxSx1_fk1 = _rec_inputs()

    def _L0_cond_setup():
        import jax, jax.numpy as jnp
        import numpy as np
        H = 16
        LN_EPS = 1e-05

        def _layernorm(x, scale, bias):
            mu = jnp.mean(x, axis=-1, keepdims=True)
            var = jnp.var(x, axis=-1, keepdims=True)
            return (x - mu) * jax.lax.rsqrt(var + LN_EPS) * scale + bias
        key = jax.random.key(seed)
        ks = jax.random.split(key, 8)
        B, T, D, E = (4, 2048, 512, 1024)
        s = 0.02
        return {'x': jax.random.normal(ks[0], (B, T, D), jnp.float32), 'emb': jax.random.normal(ks[1], (B, E), jnp.float32), 'src_mask': jax.random.randint(ks[2], (B, T), 0, 2).astype(jnp.int32), 'norm_scale': jnp.ones((D,), jnp.float32), 'norm_bias': jnp.zeros((D,), jnp.float32), 'Wq': jax.random.normal(ks[3], (D, D), jnp.float32) * s, 'bq': jnp.zeros((D,), jnp.float32), 'Wk': jax.random.normal(ks[4], (D, D), jnp.float32) * s, 'bk': jnp.zeros((D,), jnp.float32), 'Wv': jax.random.normal(ks[5], (D, D), jnp.float32) * s, 'bv': jnp.zeros((D,), jnp.float32), 'film_emb_W': jax.random.normal(ks[6], (E, 2 * D), jnp.float32) * s, 'film_emb_b': jnp.zeros((2 * D,), jnp.float32), 'film_norm_scale': jnp.ones((D,), jnp.float32), 'film_norm_bias': jnp.zeros((D,), jnp.float32), 'film_out_W': jax.random.normal(ks[7], (D, D), jnp.float32) * s, 'film_out_b': jnp.zeros((D,), jnp.float32)}
    _L0_cond_all = _L0_cond_setup()
    _L0_cond_in = {k: v for k, v in _L0_cond_all.items() if k in ('norm_scale', 'norm_bias', 'Wq', 'bq', 'Wk', 'bk', 'Wv', 'bv', 'film_emb_W', 'film_emb_b', 'film_norm_scale', 'film_norm_bias', 'film_out_W', 'film_out_b')}
    del _L0_cond_all

    def _L1_cond_setup():
        import jax, jax.numpy as jnp
        import numpy as np
        B, T, D, H, TE = (4, 1024, 512, 8, 1024)
        EPS = 1e-05

        def _ln(x, w, b):
            m = jnp.mean(x, axis=-1, keepdims=True)
            v = jnp.mean((x - m) ** 2, axis=-1, keepdims=True)
            return (x - m) * jax.lax.rsqrt(v + EPS) * w + b
        key = jax.random.key(seed)
        ks = jax.random.split(key, 16)
        s = 0.02
        inp = {'x': jax.random.normal(ks[0], (B, T, D), jnp.float32), 'emb': jax.random.normal(ks[1], (B, TE), jnp.float32), 'src_mask': (jax.random.uniform(ks[2], (B, T, 1)) > 0.2).astype(jnp.float32), 'num_head': H, 'ln_w': jnp.ones((D,), jnp.float32), 'ln_b': jnp.zeros((D,), jnp.float32), 'Wq': jax.random.normal(ks[3], (D, D), jnp.float32) * s, 'bq': jnp.zeros((D,), jnp.float32), 'Wk': jax.random.normal(ks[4], (D, D), jnp.float32) * s, 'bk': jnp.zeros((D,), jnp.float32), 'Wv': jax.random.normal(ks[5], (D, D), jnp.float32) * s, 'bv': jnp.zeros((D,), jnp.float32), 'W_emb': jax.random.normal(ks[6], (TE, 2 * D), jnp.float32) * s, 'b_emb': jnp.zeros((2 * D,), jnp.float32), 'ln2_w': jnp.ones((D,), jnp.float32), 'ln2_b': jnp.zeros((D,), jnp.float32), 'W_out': jax.random.normal(ks[7], (D, D), jnp.float32) * s, 'b_out': jnp.zeros((D,), jnp.float32)}
        return inp
    _L1_cond_all = _L1_cond_setup()
    _L1_cond_in = {k: v for k, v in _L1_cond_all.items() if k in ('ln_w', 'ln_b', 'Wq', 'bq', 'Wk', 'bk', 'Wv', 'bv', 'W_emb', 'b_emb', 'ln2_w', 'ln2_b', 'W_out', 'b_out')}
    del _L1_cond_all
    return {'x': x, 'cond_2048': cond_2048, 'mask_BxS_ik0': mask_BxS_ik0, 'mask_BxSx1_fk1': mask_BxSx1_fk1, 'L0_cond_norm_scale': _L0_cond_in['norm_scale'], 'L0_cond_norm_bias': _L0_cond_in['norm_bias'], 'L0_cond_Wq': _L0_cond_in['Wq'], 'L0_cond_bq': _L0_cond_in['bq'], 'L0_cond_Wk': _L0_cond_in['Wk'], 'L0_cond_bk': _L0_cond_in['bk'], 'L0_cond_Wv': _L0_cond_in['Wv'], 'L0_cond_bv': _L0_cond_in['bv'], 'L0_cond_film_emb_W': _L0_cond_in['film_emb_W'], 'L0_cond_film_emb_b': _L0_cond_in['film_emb_b'], 'L0_cond_film_norm_scale': _L0_cond_in['film_norm_scale'], 'L0_cond_film_norm_bias': _L0_cond_in['film_norm_bias'], 'L0_cond_film_out_W': _L0_cond_in['film_out_W'], 'L0_cond_film_out_b': _L0_cond_in['film_out_b'], 'L1_cond_ln_w': _L1_cond_in['ln_w'], 'L1_cond_ln_b': _L1_cond_in['ln_b'], 'L1_cond_Wq': _L1_cond_in['Wq'], 'L1_cond_bq': _L1_cond_in['bq'], 'L1_cond_Wk': _L1_cond_in['Wk'], 'L1_cond_bk': _L1_cond_in['bk'], 'L1_cond_Wv': _L1_cond_in['Wv'], 'L1_cond_bv': _L1_cond_in['bv'], 'L1_cond_W_emb': _L1_cond_in['W_emb'], 'L1_cond_b_emb': _L1_cond_in['b_emb'], 'L1_cond_ln2_w': _L1_cond_in['ln2_w'], 'L1_cond_ln2_b': _L1_cond_in['ln2_b'], 'L1_cond_W_out': _L1_cond_in['W_out'], 'L1_cond_b_out': _L1_cond_in['b_out']}

def reference(x, cond_2048, mask_BxS_ik0, mask_BxSx1_fk1, L0_cond_norm_scale, L0_cond_norm_bias, L0_cond_Wq, L0_cond_bq, L0_cond_Wk, L0_cond_bk, L0_cond_Wv, L0_cond_bv, L0_cond_film_emb_W, L0_cond_film_emb_b, L0_cond_film_norm_scale, L0_cond_film_norm_bias, L0_cond_film_out_W, L0_cond_film_out_b, L1_cond_ln_w, L1_cond_ln_b, L1_cond_Wq, L1_cond_bq, L1_cond_Wk, L1_cond_bk, L1_cond_Wv, L1_cond_bv, L1_cond_W_emb, L1_cond_b_emb, L1_cond_ln2_w, L1_cond_ln2_b, L1_cond_W_out, L1_cond_b_out):
    import jax
    import jax.numpy as jnp

    def _L0_cond_ref(x, emb, src_mask, norm_scale, norm_bias, Wq, bq, Wk, bk, Wv, bv, film_emb_W, film_emb_b, film_norm_scale, film_norm_bias, film_out_W, film_out_b):
        import jax, jax.numpy as jnp
        import numpy as np
        H = 16
        LN_EPS = 1e-05

        def _layernorm(x, scale, bias):
            mu = jnp.mean(x, axis=-1, keepdims=True)
            var = jnp.var(x, axis=-1, keepdims=True)
            return (x - mu) * jax.lax.rsqrt(var + LN_EPS) * scale + bias
        B, T, D = x.shape
        dh = D // H
        xn = _layernorm(x, norm_scale, norm_bias)
        q = xn @ Wq + bq
        k = xn @ Wk + bk
        v = xn @ Wv + bv
        mask = (src_mask == 1)[:, :, None]
        k = jnp.where(mask, -jnp.inf, k)
        v = jnp.where(mask, 0.0, v)
        q = q.reshape(B, T, H, dh).transpose(0, 2, 1, 3)
        k = k.reshape(B, T, H, dh).transpose(0, 2, 1, 3)
        v = v.reshape(B, T, H, dh).transpose(0, 2, 1, 3)
        q = jax.nn.softmax(q, axis=-1)
        k = jax.nn.softmax(k, axis=2)
        attn = jnp.einsum('bhse,bhsd->bhed', k, v)
        y = jnp.einsum('bhtd,bhed->bhte', q, attn)
        y = y.transpose(0, 2, 1, 3).reshape(B, T, D)
        emb_out = jax.nn.silu(emb) @ film_emb_W + film_emb_b
        scale, shift = jnp.split(emb_out, 2, axis=-1)
        h = _layernorm(y, film_norm_scale, film_norm_bias) * (1.0 + scale[:, None, :]) + shift[:, None, :]
        h = jax.nn.silu(h) @ film_out_W + film_out_b
        return x + h

    def _L1_cond_ref(x, emb, src_mask, num_head, ln_w, ln_b, Wq, bq, Wk, bk, Wv, bv, W_emb, b_emb, ln2_w, ln2_b, W_out, b_out):
        import jax, jax.numpy as jnp
        import numpy as np
        B, T, D, H, TE = (4, 1024, 512, 8, 1024)
        EPS = 1e-05

        def _ln(x, w, b):
            m = jnp.mean(x, axis=-1, keepdims=True)
            v = jnp.mean((x - m) ** 2, axis=-1, keepdims=True)
            return (x - m) * jax.lax.rsqrt(v + EPS) * w + b
        b, t, d = x.shape
        h = num_head
        dh = d // h
        xn = _ln(x, ln_w, ln_b)
        q = xn @ Wq + bq
        k = xn @ Wk + bk + (1.0 - src_mask) * -1000000.0
        q = jax.nn.softmax(q.reshape(b, t, h, dh), axis=-1)
        k = jax.nn.softmax(k.reshape(b, t, h, dh), axis=1)
        v = ((xn @ Wv + bv) * src_mask).reshape(b, t, h, dh)
        att = jnp.einsum('bnhd,bnhl->bhdl', k, v)
        y = jnp.einsum('bnhd,bhdl->bnhl', q, att).reshape(b, t, d)
        emb_out = (jax.nn.silu(emb) @ W_emb + b_emb)[:, None, :]
        scale, shift = jnp.split(emb_out, 2, axis=2)
        hh = _ln(y, ln2_w, ln2_b) * (1.0 + scale) + shift
        hh = jax.nn.silu(hh) @ W_out + b_out
        return x + hh
    x = _L0_cond_ref(x, cond_2048, mask_BxS_ik0, L0_cond_norm_scale, L0_cond_norm_bias, L0_cond_Wq, L0_cond_bq, L0_cond_Wk, L0_cond_bk, L0_cond_Wv, L0_cond_bv, L0_cond_film_emb_W, L0_cond_film_emb_b, L0_cond_film_norm_scale, L0_cond_film_norm_bias, L0_cond_film_out_W, L0_cond_film_out_b)
    x = _L1_cond_ref(x, cond_2048, mask_BxSx1_fk1, 8, L1_cond_ln_w, L1_cond_ln_b, L1_cond_Wq, L1_cond_bq, L1_cond_Wk, L1_cond_bk, L1_cond_Wv, L1_cond_bv, L1_cond_W_emb, L1_cond_b_emb, L1_cond_ln2_w, L1_cond_ln2_b, L1_cond_W_out, L1_cond_b_out)
    return x

_drawn_inputs = setup_inputs


def setup_inputs(seed=0):
    import zlib

    import numpy as np

    out = dict(_drawn_inputs(seed))
    spreads = {'L0_cond_norm_scale': (1.0, 0.2),
     'L0_cond_norm_bias': (0.0, 0.1),
     'L0_cond_bq': (0.0, 0.1),
     'L0_cond_bk': (0.0, 0.8),
     'L0_cond_bv': (0.0, 0.1),
     'L0_cond_film_emb_b': (0.0, 0.1),
     'L0_cond_film_norm_scale': (1.0, 0.2),
     'L0_cond_film_norm_bias': (0.0, 0.1),
     'L0_cond_film_out_b': (0.0, 0.1),
     'L1_cond_ln_w': (1.0, 0.2),
     'L1_cond_ln_b': (0.0, 0.1),
     'L1_cond_bq': (0.0, 0.8),
     'L1_cond_bk': (0.0, 0.8),
     'L1_cond_bv': (0.0, 0.1),
     'L1_cond_b_emb': (0.0, 0.1),
     'L1_cond_ln2_w': (1.0, 0.2),
     'L1_cond_ln2_b': (0.0, 0.29),
     'L1_cond_b_out': (0.0, 0.1)}
    factors = {'L1_cond_Wq': 8.0, 'L1_cond_Wk': 8.0}
    for name, (base, spread) in spreads.items():
        noise = np.random.default_rng([zlib.crc32(name.encode()), seed]).standard_normal(out[name].shape)
        drawn = base * np.exp(spread * noise) if base else spread * noise
        out[name] = jnp.asarray(drawn.astype(out[name].dtype))
    for name, factor in factors.items():
        out[name] = (out[name] * factor).astype(out[name].dtype)
    return out
```

```python
from contextlib import ExitStack

import concourse.bass as bass
from concourse import mybir

F32 = mybir.dt.float32
F32R = mybir.dt.float32r
I32 = mybir.dt.int32
ALU = mybir.AluOpType
ACT = mybir.ActivationFunctionType
AX_X = mybir.AxisListType.X

P = 128
BATCHES, SEQ, DIM, EMB = 8, 512, 512, 1024
TILES = SEQ // P
CHUNKS = DIM // P
EMB_CHUNKS = EMB // P
LAYERS = 2
HEADS = (16, 8)
ITERS = LAYERS * BATCHES
EPS = 1e-5
MASKED_0 = -1e30
MASKED_1 = -1e6
Q, K, V, O = range(4)
RAW_ORDER = (K, V, Q, O)
VCOLS = P + 2
BCOLS = P + 4
GROUP = 256

PARAM_ROWS = ("ln_scale", "ln_bias", "bk", "film_scale", "film_bias")


def build_program(nc, a, out):
    with ExitStack() as ctx:
        def sb(name, shape, dt=F32):
            return ctx.enter_context(nc.sbuf_tensor(name, shape, dt))

        def sem(name):
            return ctx.enter_context(nc.semaphore(name))

        x_mid = nc.dram_tensor("x_between_layers", [BATCHES, SEQ, DIM], F32).ap()

        def rows(ap, b):
            return ap[b, :, :].rearrange("(p t) d -> p t d", t=TILES) if isinstance(b, int) else \
                ap[bass.ds(b, 1), :, :].rearrange("a (p t) d -> (a p) t d", t=TILES)

        source = (a["x"], x_mid)
        target = (x_mid, out)

        w_high = [sb(f"w_high_{n}", [P, CHUNKS, DIM], F32R) for n in "qkvo"]
        w_low = [sb(f"w_low_{n}", [P, CHUNKS, DIM], F32R) for n in "qkvo"]
        raw = sb("raw_weights", [P, 2 * CHUNKS, DIM])
        bias_rows = sb("bias_rows", [P, 4, DIM])
        v_bias_blocks = sb("v_bias_blocks", [P, CHUNKS, P])
        ln_bias_cols = sb("ln_bias_cols", [P, CHUNKS, P])
        bk_col = sb("bk_col", [P, CHUNKS])
        param_in = sb("param_in", [LAYERS * len(PARAM_ROWS) * CHUNKS, P])
        params = sb("params", [P, LAYERS, len(PARAM_ROWS), CHUNKS])
        ident = sb("ident", [P, P])
        ones = sb("ones", [P, P], F32R)
        head_blocks = [sb(f"head_blocks_{n}", [P, P]) for n in range(LAYERS)]
        eps_pow = sb("minus_half", [P, TILES])
        masked_in = sb("masked_in", [P, BATCHES, TILES], I32)
        k_mask = sb("k_mask", [P, ITERS, TILES])
        v_mask = sb("v_mask", [P, ITERS, TILES])
        sum_mask = sb("sum_mask", [P, ITERS, TILES])
        film_scale = sb("film_scale", [P, ITERS, CHUNKS])
        film_shift = sb("film_shift", [P, ITERS, CHUNKS])

        x_in = sb("x_in", [P, TILES, DIM])
        x_res = sb("x_res", [P, TILES, DIM])
        x_stats = sb("x_stats", [P, TILES, 6])
        x_moments = sb("x_moments", [P, TILES, 2])
        x_var = sb("x_var", [P, TILES])
        x_rstd = sb("x_rstd", [P, TILES])
        xT_high = sb("xT_high", [P, CHUNKS, SEQ], F32R)
        xT_low = sb("xT_low", [P, CHUNKS, SEQ], F32R)
        k_max = sb("k_max", [P, DIM])
        k_top = sb("k_top", [P, 3, CHUNKS])
        k_shift = sb("k_shift", [P, CHUNKS, P], F32R)
        k_exp = sb("k_exp", [P, TILES, DIM])
        v = sb("v", [P, TILES, CHUNKS, VCOLS])
        q = sb("q", [P, TILES, DIM])
        q_max = sb("q_max", [P, TILES, HEADS[0]])
        qT = sb("qT", [P, TILES, CHUNKS, P])
        att_sums = sb("att_sums", [P, CHUNKS, 2])
        att_scale = sb("att_scale", [P, 2, CHUNKS])
        att = sb("att", [P, CHUNKS, BCOLS])
        q_rsum = sb("q_rsum", [P, TILES, HEADS[0]])
        y = sb("y", [P, TILES, DIM])
        y_stats = sb("y_stats", [P, TILES, 6])
        y_moments = sb("y_moments", [P, TILES, 2])
        y_var = sb("y_var", [P, TILES])
        y_rstd = sb("y_rstd", [P, TILES])
        gate = sb("gate", [P, 2, SEQ])
        gT_high = sb("gT_high", [P, CHUNKS, SEQ], F32R)
        gT_low = sb("gT_low", [P, CHUNKS, SEQ], F32R)

        emb = gate[0:BATCHES, :, :].rearrange("p a n -> p (a n)")
        embT = sb("embT", [P, EMB_CHUNKS, BATCHES])
        film_row = sb("film_row", [BATCHES, 2 * DIM])
        film_bias_row = sb("film_bias_row", [BATCHES, LAYERS, 2 * DIM])

        psum_t = ctx.enter_context(nc.psum_tensor("psum_t", [P, 2, CHUNKS, P], F32))
        psum_w = ctx.enter_context(nc.psum_tensor("psum_w", [P, 2, DIM], F32))
        psum_k = ctx.enter_context(nc.psum_tensor("psum_k", [P, TILES, DIM], F32))
        quads = psum_k[:, :, :].rearrange("p a (b n) -> p (a b) n", n=GROUP)
        att_turned_psum = psum_k[:, 0, :].rearrange("p (g n) -> p g n", n=P)
        att_psum = quads[:, 0:CHUNKS, :]

        def y_psum_of(t):
            at = CHUNKS * (1 - t % 2)
            return quads[:, at:at + CHUNKS, :]

        params_loaded, params_turned, params_ready = sem("params_loaded"), sem("params_turned"), sem("params_ready")
        masks_loaded, consts_step, masks_step = sem("masks_loaded"), sem("consts_step"), sem("masks_step")
        emb_loaded, emb_silu, emb_turned, embT_ready = (
            sem("emb_loaded"), sem("emb_silu"), sem("emb_turned"), sem("embT_ready"))
        film_loaded, film_psum, film_added, film_turned, film_step = (
            sem("film_loaded"), sem("film_psum"), sem("film_added"), sem("film_turned"), sem("film_step"))
        raw_loaded = [sem("raw_loaded_0"), sem("raw_loaded_1")]
        bias_loaded, ln_bias_ready = sem("bias_loaded"), sem("ln_bias_ready")
        w_high_ready, w_low_ready = sem("w_high_ready"), sem("w_low_ready")
        bias_psum, bias_ready, bk_turned, bk_ready = (
            sem("bias_psum"), sem("bias_ready"), sem("bk_turned"), sem("bk_ready"))
        x_loaded, x_stats_done, x_moments_done, x_scale_done, xn_ready = (
            sem("x_loaded"), sem("x_stats_done"), sem("x_moments_done"), sem("x_scale_done"), sem("xn_ready"))
        xT_psum, xT_high_ready, xT_low_ready = sem("xT_psum"), sem("xT_high_ready"), sem("xT_low_ready")
        k_psum, k_max_done, k_max_turned, k_top_step, k_shift_ready, k_shifted, k_exp_ready = (
            sem("k_psum"), sem("k_max_done"), sem("k_max_turned"), sem("k_top_step"),
            sem("k_shift_ready"), sem("k_shifted"), sem("k_exp_ready"))
        v_psum, v_ready, v_masks_ready = sem("v_psum"), sem("v_ready"), sem("v_masks_ready")
        q_psum, q_biased, q_max_done, q_shifted, q_exp_ready = (
            sem("q_psum"), sem("q_biased"), sem("q_max_done"), sem("q_shifted"), sem("q_exp_ready"))
        att_done, att_step, att_built, att_turned, att_ready, att_ones_ready = (
            sem("att_done"), sem("att_step"), sem("att_built"), sem("att_turned"), sem("att_ready"),
            sem("att_ones_ready"))
        qT_psum, qT_ready = sem("qT_psum"), sem("qT_ready")
        y_psum, q_rsum_done, y_ready, y_stats_done, y_moments_done, y_scale_done, yn_ready = (
            sem("y_psum"), sem("q_rsum_done"), sem("y_ready"), sem("y_stats_done"),
            sem("y_moments_done"), sem("y_scale_done"), sem("yn_ready"))
        yT_psum, gate_ready, g_high_ready, g_low_ready = (
            sem("yT_psum"), sem("gate_ready"), sem("g_high_ready"), sem("g_low_ready"))
        o_psum, res_loaded, res_biased, o_added, stored = (
            sem("o_psum"), sem("res_loaded"), sem("res_biased"), sem("o_added"), sem("stored"))

        waits_passed = sem("waits_passed")
        ATT_STEPS = 3 + CHUNKS
        FILM_STEPS = 4
        FILM_PER_LAYER = 2

        block = ctx.enter_context(nc.Block())

        def wait_apart(eng, semaphore, value):
            eng.wait_ge(semaphore, value)
            eng.sem_inc(waits_passed, 1)

        def run_layers(eng, start_layer, iteration, output_stage, middle=None):
            for layer in range(LAYERS):
                first, last = layer * BATCHES, layer * BATCHES + BATCHES - 1
                start_layer(layer)
                iteration(layer, first, False, True)
                if middle is not None and layer == 0:
                    middle()
                with eng.Fori(first + 1, last) as i:
                    iteration(layer, i, True, True)
                iteration(layer, last, True, last + 1 < ITERS)
                output_stage(layer, last)

        @block.sync
        def _(sp):
            def load_raw(layer, n, slot, weights):
                sp.dma_start(raw[:, slot * CHUNKS:(slot + 1) * CHUNKS, :],
                             weights.rearrange("(c p) n -> p c n", p=P)).then_inc(raw_loaded[slot], 16)

            def weights_of(layer, m):
                return a[("L0_cond_", "L1_cond_")[layer] + NAMES[layer][m]]

            def load_x(i, layer):
                if layer:
                    sp.wait_ge(stored, 16 * (i - BATCHES + 1))
                sp.dma_start(x_in[:, :, :], rows(source[layer], i - BATCHES * layer)).then_inc(x_loaded, 16)

            def load_biases(layer):
                for m in (Q, K, V, O):
                    row = a[("L0_cond_", "L1_cond_")[layer] + BIAS_NAMES[layer][m]]
                    sp.dma_start(bias_rows[:, m, :], row.partition_broadcast(P)).then_inc(bias_loaded, 16)

            def load_weights(layer, orders):
                for n in orders:
                    if n >= 2:
                        sp.wait_ge(w_low_ready, CHUNKS * (4 * layer + n - 1))
                        sp.wait_ge(bias_psum, 3 * layer + n - 1)
                    load_raw(layer, n, n % 2, weights_of(layer, RAW_ORDER[n]))

            load_x(0, 0)
            load_weights(0, (0, 1))
            for layer in range(LAYERS):
                for r, key in enumerate(PARAM_ROWS):
                    at = (layer * len(PARAM_ROWS) + r) * CHUNKS
                    sp.dma_start(param_in[at:at + CHUNKS, :],
                                 a[PARAM_NAMES[layer][r]].rearrange("(c p) -> c p", p=P)).then_inc(params_loaded, 16)
            load_biases(0)
            sp.dma_start(masked_in[:, :, :], a["mask_BxS_ik0"].rearrange("b (p t) -> p b t", t=TILES))\
              .then_inc(masks_loaded, 16)
            sp.dma_start(v_mask[:, BATCHES:ITERS, :],
                         a["mask_BxSx1_fk1"].rearrange("b (p t) o -> p b (t o)", t=TILES)).then_inc(masks_loaded, 16)
            load_weights(0, (2, 3))
            sp.dma_start(emb, a["cond_2048"]).then_inc(emb_loaded, 16)
            for layer, name in enumerate(("L0_cond_film_emb_b", "L1_cond_b_emb")):
                sp.dma_start(film_bias_row[:, layer, :], a[name].partition_broadcast(BATCHES))\
                  .then_inc(emb_loaded, 16)

            def middle():
                for n in range(2 * LAYERS):
                    layer, half = n // 2, n % 2
                    if n == 0:
                        sp.wait_ge(w_low_ready, CHUNKS * 4)
                        sp.wait_ge(bias_psum, 3)
                    else:
                        sp.wait_ge(film_psum, n)
                    sp.dma_start(raw[:, :, :],
                                 a[("L0_cond_film_emb_W", "L1_cond_W_emb")[layer]]
                                 [:, half * DIM:(half + 1) * DIM].rearrange("(c p) n -> p c n", p=P))\
                      .then_inc(film_loaded, 16)
                sp.wait_ge(film_psum, 2 * LAYERS)
                load_weights(1, (0, 1))

            def iteration(layer, i, with_output, with_next):
                if with_next:
                    sp.wait_ge(xT_psum, TILES * (i + 1))
                    next_layer = 1 if isinstance(i, int) and i + 1 >= BATCHES else layer
                    load_x(i + 1, next_layer)
                if with_output:
                    output_stage(layer, i - 1)

            def output_stage(layer, j):
                sp.dma_start(x_res[:, :, :], rows(source[layer], j - BATCHES * layer)).then_inc(res_loaded, 16)
                sp.wait_ge(o_added, TILES * (j + 1))
                sp.dma_start(rows(target[layer], j - BATCHES * layer), x_res[:, :, :]).then_inc(stored, 16)
                wait_apart(sp, stored, 16 * (j + 1))

            def start_layer(layer):
                if layer:
                    sp.wait_ge(o_added, TILES * BATCHES)
                    sp.wait_ge(res_biased, TILES * BATCHES)
                    sp.wait_ge(att_ready, BATCHES)
                    load_biases(1)
                    load_weights(1, (2, 3))

            run_layers(sp, start_layer, iteration, output_stage, middle)
            sp.wait_ge(stored, 16 * ITERS)

        @block.tensor
        def _(pe):
            def split_product(dst, lhs_high, lhs_low, rhs_high, rhs_low):
                for c in range(CHUNKS):
                    for n, (lhs, rhs) in enumerate(((lhs_high, rhs_high), (lhs_high, rhs_low), (lhs_low, rhs_high))):
                        last = pe.matmul(dst, lhs(c), rhs[:, c, :], start=(c == 0 and n == 0),
                                         stop=(c == CHUNKS - 1 and n == 2))
                return last

            def project(dst, t, m):
                return split_product(dst, lambda c: xT_high[:, c, t * P:(t + 1) * P],
                                     lambda c: xT_low[:, c, t * P:(t + 1) * P], w_high[m], w_low[m])

            def start_layer(layer):
                if layer == 0:
                    pe.wait_ge(params_loaded, 16 * LAYERS * len(PARAM_ROWS))
                    pe.wait_ge(consts_step, 2)
                    n = LAYERS * len(PARAM_ROWS) * CHUNKS
                    pe.transpose(psum_t[:, 0, 0, 0:n], param_in[:, :], ident[0:n, 0:n]).then_inc(params_turned, 1)
                pe.wait_ge(ln_bias_ready, layer + 1)
                if layer:
                    pe.wait_ge(o_added, TILES * BATCHES * layer)
                for n, m in enumerate(RAW_ORDER[:3]):
                    slot = n % 2
                    pe.wait_ge(raw_loaded[slot], 16 * (2 * layer + n // 2 + 1))
                    if n >= 2:
                        pe.wait_ge(bias_ready, 3 * layer + n - 1)
                    for c in range(CHUNKS):
                        mm = pe.matmul(psum_w[:, n % 2, :], ln_bias_cols[:, c, :], raw[:, slot * CHUNKS + c, :],
                                       start=(c == 0), stop=(c == CHUNKS - 1))
                    mm.then_inc(bias_psum, 1)
                    if n == 0:
                        pe.wait_ge(bias_ready, 3 * layer + 1)
                        pe.wait_ge(params_ready, 1)
                        for c in range(CHUNKS):
                            mm = pe.transpose(psum_t[:, 0, c, :], bias_rows[:, K, c * P:(c + 1) * P], ident[:, :])
                        mm.then_inc(bk_turned, 1)
                pe.wait_ge(bias_ready, 3 * layer + 3)
                pe.wait_ge(bk_ready, layer + 1)

            def middle():
                pe.wait_ge(emb_silu, 1)
                pe.wait_ge(qT_ready, TILES)
                for c in range(EMB_CHUNKS):
                    mm = pe.transpose(psum_t[:, 0, 0, c * BATCHES:(c + 1) * BATCHES],
                                      emb[:, c * P:(c + 1) * P], ident[0:BATCHES, 0:BATCHES])
                mm.then_inc(emb_turned, 1)
                pe.wait_ge(embT_ready, 1)
                pe.wait_ge(q_biased, TILES)
                for n in range(2 * LAYERS):
                    pe.wait_ge(film_loaded, 16 * (n + 1))
                    if n >= 2:
                        pe.wait_ge(film_added, n - 1)
                    for c in range(EMB_CHUNKS):
                        mm = pe.matmul(psum_w[0:BATCHES, n % 2, :], embT[:, c, :], raw[:, c, :],
                                       start=(c == 0), stop=(c == EMB_CHUNKS - 1))
                    mm.then_inc(film_psum, 1)
                    if n % 2:
                        layer = n // 2
                        pe.wait_ge(film_added, 2 * layer + 2)
                        if layer:
                            pe.wait_ge(film_step, FILM_STEPS * layer)
                        for c in range(2 * CHUNKS):
                            mm = pe.transpose(psum_t[:, 0, 0, c * BATCHES:(c + 1) * BATCHES],
                                              film_row[:, c * P:(c + 1) * P], ident[0:BATCHES, 0:BATCHES])
                        mm.then_inc(film_turned, 1)
                pe.wait_ge(film_step, FILM_STEPS * LAYERS)

            def turn_y(j, c):
                if c == 0:
                    pe.wait_ge(yn_ready, TILES * (j + 1))
                if c < 2:
                    pe.wait_ge(xT_low_ready, TILES * (j + 1))
                else:
                    pe.wait_ge(gate_ready, CHUNKS * j + c - 1)
                for t in range(TILES):
                    mm = pe.transpose(psum_t[:, c % 2, t, :], y[:, t, c * P:(c + 1) * P], ident[:, :])
                mm.then_inc(yT_psum, 1)

            def out_projection(j, t, alone=False):
                if t == 0:
                    pe.wait_ge(g_low_ready, CHUNKS * (j + 1))
                if t < 2:
                    pe.wait_ge(q_biased, TILES * (j + (1 if alone else 2)) )
                else:
                    pe.wait_ge(o_added, TILES * j + t - 1)
                split_product(psum_w[:, t % 2, :], lambda c: gT_high[:, c, t * P:(t + 1) * P],
                              lambda c: gT_low[:, c, t * P:(t + 1) * P], w_high[O], w_low[O]).then_inc(o_psum, 1)

            def output_stage(layer, j):
                for c in range(CHUNKS):
                    turn_y(j, c)
                for t in range(TILES):
                    out_projection(j, t, alone=True)

            def iteration(layer, i, with_output, with_next):
                first = not with_output
                if first:
                    pe.wait_ge(w_high_ready, CHUNKS * 4 * (layer + 1))
                    pe.wait_ge(w_low_ready, CHUNKS * 4 * (layer + 1))
                for t in range(TILES):
                    pe.wait_ge(xn_ready, TILES * i + t + 1)
                    if t >= 2:
                        pe.wait_ge(xT_low_ready, TILES * i + t - 1)
                    elif not (first and layer == 0):
                        pe.wait_ge(qT_ready, TILES * (i - 1) + t + 3)
                    for c in range(CHUNKS):
                        mm = pe.transpose(psum_t[:, t % 2, c, :], x_in[:, t, c * P:(c + 1) * P], ident[:, :])
                    mm.then_inc(xT_psum, 1)
                for t in range(TILES):
                    pe.wait_ge(xT_low_ready, TILES * i + t + 1)
                    if t == 0 and not (first and layer == 0):
                        pe.wait_ge(y_ready, TILES * i)
                    project(psum_k[:, t, :], t, K).then_inc(k_psum, 1)

                def v_projection(t):
                    if t >= 2:
                        pe.wait_ge(v_ready, TILES * i + t - 1)
                    project(psum_w[:, t % 2, :], t, V).then_inc(v_psum, 1)

                if with_output:
                    turn_y(i - 1, 0)
                    turn_y(i - 1, 1)
                v_projection(0)
                if with_output:
                    turn_y(i - 1, 2)
                    turn_y(i - 1, 3)
                v_projection(1)
                pe.wait_ge(k_max_done, TILES * (i + 1))
                if with_output:
                    pe.wait_ge(gate_ready, CHUNKS * (i - 1) + 3)
                else:
                    pe.wait_ge(xT_low_ready, TILES * i + 3)
                for c in range(CHUNKS):
                    mm = pe.transpose(psum_t[:, 0, c, :], k_max[:, c * P:(c + 1) * P], ident[:, :])
                mm.then_inc(k_max_turned, 1)
                v_projection(2)
                pe.wait_ge(k_shift_ready, i + 1)
                for t in range(TILES):
                    pe.matmul(psum_k[:, t, :], ones[:, :], k_shift[:, :, :].rearrange("p c n -> p (c n)"),
                              start=False, stop=True, skip_group_check=True).then_inc(k_shifted, 1)
                v_projection(3)
                for t in range(TILES):
                    if t < 2:
                        pe.wait_ge(v_ready, TILES * i + t + 3)
                    else:
                        pe.wait_ge(q_biased, TILES * i + t - 1)
                    project(psum_w[:, t % 2, :], t, Q).then_inc(q_psum, 1)
                pe.wait_ge(k_exp_ready, TILES * (i + 1))
                pe.wait_ge(v_ready, TILES * (i + 1))
                pe.wait_ge(v_masks_ready, 2 * (i + 1))
                for g in range(CHUNKS):
                    for t in range(TILES):
                        mm = pe.matmul(att_psum[:, g, 0:VCOLS], k_exp[:, t, g * P:(g + 1) * P], v[:, t, g, :],
                                       start=(t == 0), stop=(t == TILES - 1))
                mm.then_inc(att_done, 1)

                def turn_att():
                    pe.wait_ge(att_built, i + 1)
                    for g in range(CHUNKS):
                        mm = pe.transpose(att_turned_psum[:, g, :], att[:, g, 0:P], ident[:, :])
                    mm.then_inc(att_turned, 1)

                if with_output:
                    out_projection(i - 1, 0)
                    out_projection(i - 1, 1)
                if layer == 0:
                    turn_att()
                if with_output:
                    out_projection(i - 1, 2)
                    out_projection(i - 1, 3)

                def turn_q(t):
                    pe.wait_ge(q_exp_ready, TILES * i + t + 1)
                    if t == 0:
                        pe.wait_ge(k_top_step, 3 * i + 1)
                    elif t == 1:
                        if with_output:
                            pe.wait_ge(gate_ready, CHUNKS * i)
                        else:
                            pe.wait_ge(xT_low_ready, TILES * i + 4)
                    else:
                        pe.wait_ge(qT_ready, TILES * i + t - 1)
                    for c in range(CHUNKS):
                        mm = pe.transpose(psum_t[:, t % 2, c, :], q[:, t, c * P:(c + 1) * P], ident[:, :])
                    mm.then_inc(qT_psum, 1)

                def attend(t):
                    pe.wait_ge(qT_ready, TILES * i + t + 1)
                    if t == 0:
                        pe.wait_ge(att_ready, i + 1)
                    if t >= 2:
                        pe.wait_ge(y_ready, TILES * i + t - 1)
                    for g in range(CHUNKS):
                        mm = pe.matmul(y_psum_of(t)[:, g, 0:BCOLS], qT[:, t, g, :], att[:, g, :],
                                       start=True, stop=True)
                    mm.then_inc(y_psum, 1)

                turn_q(0)
                turn_q(1)
                attend(0)
                turn_q(2)
                attend(1)
                turn_q(3)
                attend(2)
                attend(3)

            run_layers(pe, start_layer, iteration, output_stage, middle)

        @block.vector
        def _(dve):
            def next_x(i):
                dve.wait_ge(x_loaded, 16 * (i + 1))
                for t in range(TILES):
                    dve.bn_stats(x_stats[:, t, :], x_in[:, t, :]).then_inc(x_stats_done, 1)
                for t in range(TILES):
                    wait_apart(dve, x_stats_done, TILES * i + t + 1)
                    dve.bn_aggr(x_moments[:, t, :], x_stats[:, t, :]).then_inc(x_moments_done, 1)

            def next_xn(i):
                dve.wait_ge(x_scale_done, 2 * (i + 1))
                dve.wait_ge(x_moments_done, TILES * (i + 1))
                for t in range(TILES):
                    dve.tensor_scalar(x_in[:, t, :], x_in[:, t, :], x_moments[:, t, 0:1], x_rstd[:, t:t + 1],
                                      ALU.subtract, ALU.mult).then_inc(xn_ready, 1)

            def start_layer(layer):
                if layer == 0:
                    dve.memset(eps_pow[:, :], -0.5).then_inc(masks_step, 1)
                    dve.memset(sum_mask[:, BATCHES:ITERS, :], 1.0).then_inc(masks_step, 1)
                    dve.wait_ge(masks_loaded, 32)
                    m0, m1 = slice(0, BATCHES), slice(BATCHES, ITERS)
                    dve.tensor_scalar(k_mask[:, m0, :], masked_in[:, :, :], 1.0, MASKED_0,
                                      ALU.is_equal, ALU.mult).then_inc(masks_step, 1)
                    dve.tensor_scalar(v_mask[:, m0, :], masked_in[:, :, :], 1.0, None,
                                      ALU.not_equal).then_inc(masks_step, 1)
                    dve.tensor_scalar(sum_mask[:, m0, :], masked_in[:, :, :], 1.0, None,
                                      ALU.not_equal).then_inc(masks_step, 1)
                    dve.tensor_scalar(k_mask[:, m1, :], v_mask[:, m1, :], -1.0, 1.0,
                                      ALU.mult, ALU.add).then_inc(masks_step, 1)
                    dve.wait_ge(masks_step, 6)
                    dve.tensor_scalar(k_mask[:, m1, :], k_mask[:, m1, :], MASKED_1, None,
                                      ALU.mult).then_inc(masks_step, 1)
                    dve.wait_ge(params_turned, 1)
                    dve.tensor_copy(params[:, :, :, :].rearrange("p l r c -> p (l r c)"),
                                    psum_t[:, 0, 0, 0:LAYERS * len(PARAM_ROWS) * CHUNKS]).then_inc(params_ready, 1)
                    dve.wait_ge(params_ready, 1)
                dve.tensor_copy(ln_bias_cols[:, :, :],
                                params[:, layer, 1, :].unsqueeze(2).to_broadcast([P, CHUNKS, P]))\
                   .then_inc(ln_bias_ready, 1)
                if layer == 0:
                    next_x(0)
                dve.wait_ge(bias_loaded, 16 * 4 * (layer + 1))
                for n, m in enumerate(RAW_ORDER):
                    if m != O:
                        dve.wait_ge(bias_psum, 3 * layer + n + 1)
                        dve.tensor_tensor(bias_rows[:, m, :], bias_rows[:, m, :], psum_w[:, n % 2, :],
                                          ALU.add).then_inc(bias_ready, 1)
                    for c in range(CHUNKS):
                        dve.wait_ge(w_high_ready, CHUNKS * (4 * layer + n) + c + 1)
                        scale = 1.0 if m == O else params[:, layer, 0, c:c + 1]
                        dve.scalar_tensor_tensor(out=w_low[m][:, c, :], in0=raw[:, n % 2 * CHUNKS + c, :],
                                                 scalar=scale, in1=w_high[m][:, c, :], op0=ALU.mult,
                                                 op1=ALU.subtract).then_inc(w_low_ready, 1)
                    if n == 0:
                        dve.wait_ge(bk_turned, layer + 1)
                        dve.tensor_copy(bk_col[:, :], psum_t[:, 0, :, 0]).then_inc(bk_ready, 1)
                if layer == 0:
                    next_xn(0)

            def middle():
                dve.wait_ge(emb_turned, 1)
                dve.tensor_copy(embT[:, :, :].rearrange("p c b -> p (c b)"),
                                psum_t[:, 0, 0, 0:EMB_CHUNKS * BATCHES]).then_inc(embT_ready, 1)
                for n in range(2 * LAYERS):
                    layer, half = n // 2, n % 2
                    dve.wait_ge(film_psum, n + 1)
                    if n == 2:
                        dve.wait_ge(film_turned, 1)
                    dve.tensor_tensor(film_row[:, half * DIM:(half + 1) * DIM], psum_w[0:BATCHES, n % 2, :],
                                      film_bias_row[:, layer, half * DIM:(half + 1) * DIM], ALU.add)\
                       .then_inc(film_added, 1)
                    if half:
                        at = slice(layer * BATCHES, (layer + 1) * BATCHES)
                        scale = film_scale[:, at, :].rearrange("p b c -> p c b")
                        shift = film_shift[:, at, :].rearrange("p b c -> p c b")
                        cols = psum_t[:, 0, 0, 0:2 * CHUNKS * BATCHES].rearrange("p (h c b) -> p h c b", h=2, b=BATCHES)

                        def param(r):
                            return params[:, layer, r, :].unsqueeze(2).to_broadcast([P, CHUNKS, BATCHES])

                        at = FILM_STEPS * layer
                        dve.wait_ge(film_turned, layer + 1)
                        dve.tensor_scalar(scale, cols[:, 0], 1.0, None, ALU.add).then_inc(film_step, 1)
                        dve.wait_ge(film_step, at + 1)
                        dve.tensor_tensor(shift, scale, param(4), ALU.mult).then_inc(film_step, 1)
                        dve.wait_ge(film_step, at + 2)
                        dve.tensor_tensor(shift, shift, cols[:, 1], ALU.add).then_inc(film_step, 1)
                        dve.tensor_tensor(scale, scale, param(3), ALU.mult).then_inc(film_step, 1)

            def normalise_y(j):
                dve.wait_ge(y_scale_done, 2 * (j + 1))
                dve.wait_ge(y_moments_done, TILES * (j + 1))
                for t in range(TILES):
                    dve.tensor_scalar(y[:, t, :], y[:, t, :], y_moments[:, t, 0:1], y_rstd[:, t:t + 1],
                                      ALU.subtract, ALU.mult).then_inc(yn_ready, 1)

            def split_gate(j, c):
                dve.wait_ge(g_high_ready, CHUNKS * j + c + 1)
                dve.tensor_tensor(gT_low[:, c, :], gate[:, c % 2, :], gT_high[:, c, :], ALU.subtract)\
                   .then_inc(g_low_ready, 1)

            def add_residual(j, t):
                dve.wait_ge(o_psum, TILES * j + t + 1)
                dve.wait_ge(res_biased, TILES * j + t + 1)
                dve.tensor_tensor(x_res[:, t, :], x_res[:, t, :], psum_w[:, t % 2, :], ALU.add).then_inc(o_added, 1)

            def output_stage(layer, j):
                normalise_y(j)
                for c in range(CHUNKS):
                    split_gate(j, c)
                for t in range(TILES):
                    add_residual(j, t)

            def iteration(layer, i, with_output, with_next):
                heads = HEADS[layer]
                per_group = heads // CHUNKS
                width = DIM // heads
                for t in range(TILES):
                    dve.wait_ge(xT_high_ready, TILES * i + t + 1)
                    dve.tensor_tensor(xT_low[:, :, t * P:(t + 1) * P], psum_t[:, t % 2, :, :],
                                      xT_high[:, :, t * P:(t + 1) * P], ALU.subtract).then_inc(xT_low_ready, 1)
                if with_output:
                    normalise_y(i - 1)
                for t in range(TILES):
                    dve.wait_ge(k_psum, TILES * i + t + 1)
                    mask = k_mask[:, bass.ds(i, 1), t:t + 1].rearrange("p a t -> p (a t)")
                    if t == 0:
                        dve.tensor_scalar(k_max[:, :], psum_k[:, t, :], mask, None, ALU.add).then_inc(k_max_done, 1)
                    else:
                        dve.wait_ge(k_max_done, TILES * i + t)
                        dve.scalar_tensor_tensor(out=k_max[:, :], in0=psum_k[:, t, :], scalar=mask,
                                                 in1=k_max[:, :], op0=ALU.add, op1=ALU.max).then_inc(k_max_done, 1)
                if with_output:
                    for c in range(CHUNKS):
                        split_gate(i - 1, c)
                dve.wait_ge(k_max_turned, i + 1)
                dve.tensor_reduce(k_top[:, 0, :], psum_t[:, 0, :, :], AX_X, ALU.max).then_inc(k_top_step, 1)
                dve.wait_ge(k_top_step, 3 * i + 1)
                dve.tensor_tensor(k_top[:, 1, :], k_top[:, 0, :], bk_col[:, :], ALU.add).then_inc(k_top_step, 1)
                dve.wait_ge(k_top_step, 3 * i + 2)
                dve.tensor_tensor(k_top[:, 2, :], bk_col[:, :], k_top[:, 1, :], ALU.subtract).then_inc(k_top_step, 1)
                dve.wait_ge(k_top_step, 3 * i + 3)
                dve.tensor_tensor(k_shift[:, :, :], ident[:, :].unsqueeze(1).to_broadcast([P, CHUNKS, P]),
                                  k_top[:, 2, :].unsqueeze(2).to_broadcast([P, CHUNKS, P]), ALU.mult)\
                   .then_inc(k_shift_ready, 1)
                if with_next:
                    next_x(i + 1)
                for t in range(TILES):
                    dve.wait_ge(q_psum, TILES * i + t + 1)
                    dve.tensor_tensor(q[:, t, :], psum_w[:, t % 2, :], bias_rows[:, Q, :], ALU.add)\
                       .then_inc(q_biased, 1)
                    dve.wait_ge(q_biased, TILES * i + t + 1)
                    dve.tensor_reduce(q_max[:, t, 0:heads], q[:, t, :].rearrange("p (h e) -> p h e", e=width),
                                      AX_X, ALU.max).then_inc(q_max_done, 1)
                if with_next:
                    next_xn(i + 1)
                dve.wait_ge(att_done, i + 1)
                dve.tensor_copy(att_sums[:, :, :], att_psum[:, :, P:VCOLS]).then_inc(att_step, 1)
                dve.wait_ge(att_step, ATT_STEPS * i + 1)
                dve.reciprocal(att_scale[:, 0, :], att_sums[:, :, 0]).then_inc(att_step, 1)
                dve.wait_ge(att_step, ATT_STEPS * i + 2)
                dve.tensor_tensor(att_scale[:, 1, :], att_scale[:, 0, :], att_sums[:, :, 1], ALU.mult)\
                   .then_inc(att_step, 1)
                for g in range(CHUNKS):
                    dve.scalar_tensor_tensor(out=att[:, g, 0:P], in0=att_psum[:, g, 0:P],
                                             scalar=att_scale[:, 0, g:g + 1], in1=head_blocks[layer][:, :],
                                             op0=ALU.mult, op1=ALU.mult).then_inc(att_step, 1)
                dve.wait_ge(att_step, ATT_STEPS * (i + 1))
                for g in range(CHUNKS):
                    mm = dve.scalar_tensor_tensor(out=att[:, g, 0:P], in0=v_bias_blocks[:, g, :],
                                                  scalar=att_scale[:, 1, g:g + 1], in1=att[:, g, 0:P],
                                                  op0=ALU.mult, op1=ALU.add)
                mm.then_inc(att_ready if layer else att_built, 1)
                if with_output:
                    add_residual(i - 1, 0)
                    add_residual(i - 1, 1)
                if layer == 0:
                    dve.wait_ge(att_turned, i + 1)
                    dve.tensor_copy(att[:, :, 0:P], att_turned_psum).then_inc(att_ready, 1)
                if with_output:
                    add_residual(i - 1, 2)
                    add_residual(i - 1, 3)
                for t in range(TILES):
                    ps = y_psum_of(t)
                    rsum = q_rsum[:, t, 0:heads].rearrange("p (g h) -> p g h", g=CHUNKS)
                    dve.wait_ge(y_psum, TILES * i + t + 1)
                    dve.reciprocal(rsum, ps[:, :, P:P + per_group]).then_inc(q_rsum_done, 1)
                    dve.wait_ge(q_rsum_done, TILES * i + t + 1)
                    dve.tensor_tensor(
                        y[:, t, :].rearrange("p (g h e) -> p g h e", g=CHUNKS, h=per_group),
                        ps[:, :, 0:P].rearrange("p g (h e) -> p g h e", h=per_group),
                        rsum.unsqueeze(3).to_broadcast([P, CHUNKS, per_group, width]), ALU.mult).then_inc(y_ready, 1)
                    dve.wait_ge(y_ready, TILES * i + t + 1)
                    dve.bn_stats(y_stats[:, t, :], y[:, t, :]).then_inc(y_stats_done, 1)
                    wait_apart(dve, y_stats_done, TILES * i + t + 1)
                    dve.bn_aggr(y_moments[:, t, :], y_stats[:, t, :]).then_inc(y_moments_done, 1)

            run_layers(dve, start_layer, iteration, output_stage, middle)

        @block.scalar
        def _(act):
            def start_layer(layer):
                if layer == 0:
                    act.wait_ge(params_ready, 1)
                for n, m in enumerate(RAW_ORDER):
                    act.wait_ge(raw_loaded[n % 2], 16 * (2 * layer + n // 2 + 1))
                    for c in range(CHUNKS):
                        scale = 1.0 if m == O else params[:, layer, 0, c:c + 1]
                        act.activation(w_high[m][:, c, :], raw[:, n % 2 * CHUNKS + c, :], ACT.Copy, scale=scale)\
                           .then_inc(w_high_ready, 1)

            def middle():
                act.wait_ge(emb_loaded, 16 * (1 + LAYERS))
                act.activation(emb, emb, ACT.Silu).then_inc(emb_silu, 1)

            def activate(j, c):
                act.wait_ge(yT_psum, CHUNKS * j + c + 1)
                if c >= 2:
                    act.wait_ge(g_low_ready, CHUNKS * j + c - 1)
                cond = bass.ds(j, 1)
                act.activation(gate[:, c % 2, :], psum_t[:, c % 2, :, :].rearrange("p t s -> p (t s)"), ACT.Silu,
                               scale=film_scale[:, cond, c:c + 1].rearrange("p a c -> p (a c)"),
                               bias=film_shift[:, cond, c:c + 1].rearrange("p a c -> p (a c)")).then_inc(gate_ready, 1)
                act.wait_ge(gate_ready, CHUNKS * j + c + 1)
                act.copy(gT_high[:, c, :], gate[:, c % 2, :]).then_inc(g_high_ready, 1)

            def output_stage(layer, j):
                for c in range(CHUNKS):
                    activate(j, c)

            def iteration(layer, i, with_output, with_next):
                for t in range(TILES):
                    act.wait_ge(xT_psum, TILES * i + t + 1)
                    act.copy(xT_high[:, :, t * P:(t + 1) * P], psum_t[:, t % 2, :, :]).then_inc(xT_high_ready, 1)
                if with_output:
                    for c in range(CHUNKS):
                        activate(i - 1, c)

                def mask_v(t):
                    act.wait_ge(v_psum, TILES * i + t + 1)
                    act.activation(v[:, t, :, 0:P], psum_w[:, t % 2, :].rearrange("p (g n) -> p g n", g=CHUNKS),
                                   ACT.Copy, scale=v_mask[:, bass.ds(i, 1), t:t + 1].rearrange("p a t -> p (a t)"))\
                       .then_inc(v_ready, 1)

                if not with_output and layer == 0:
                    act.wait_ge(masks_step, 7)
                mask_v(0)
                mask_v(1)
                for t in range(TILES):
                    act.wait_ge(k_shifted, TILES * i + t + 1)
                    act.activation(k_exp[:, t, :], psum_k[:, t, :], ACT.Exp,
                                   bias=k_mask[:, bass.ds(i, 1), t:t + 1].rearrange("p a t -> p (a t)"))\
                       .then_inc(k_exp_ready, 1)
                mask_v(2)
                mask_v(3)
                for t in range(TILES):
                    act.wait_ge(q_shifted, TILES * i + t + 1)
                    act.activation(q[:, t, :], q[:, t, :], ACT.Exp).then_inc(q_exp_ready, 1)
                for t in range(TILES):
                    act.wait_ge(qT_psum, TILES * i + t + 1)
                    act.copy(qT[:, t, :, :], psum_t[:, t % 2, :, :]).then_inc(qT_ready, 1)

            run_layers(act, start_layer, iteration, output_stage, middle)

        @block.gpsimd
        def _(pool):
            def scale_of(moments, var, rstd, count, done, i):
                wait_apart(pool, count, TILES * (i + 1))
                pool.tensor_scalar(var[:, :], moments[:, :, 1], EPS, None, ALU.add).then_inc(done, 1)
                pool.wait_ge(done, 2 * i + 1)
                pool.tensor_tensor(rstd[:, :], var[:, :], eps_pow[:, :], ALU.pow).then_inc(done, 1)

            def start_layer(layer):
                heads = HEADS[layer]
                width = DIM // heads
                if layer == 0:
                    pool.memset(ident[:, :], 0.0).then_inc(consts_step, 1)
                    pool.wait_ge(consts_step, 1)
                    pool.affine_select(out=ident[:, :], in_=ident[:, :], compare_op=ALU.not_equal, fill=1.0,
                                       base=0, pattern=[[-1, P]], channel_multiplier=1).then_inc(consts_step, 1)
                    pool.memset(ones[:, :].bitcast(F32), 1.0).then_inc(consts_step, 1)
                if layer:
                    pool.wait_ge(y_psum, TILES * BATCHES * layer)
                pool.memset(head_blocks[layer][:, :], 0.0).then_inc(att_ones_ready, 1)
                pool.memset(att[:, :, :], 0.0).then_inc(att_ones_ready, 1)
                pool.wait_ge(att_ones_ready, 2 * layer * 2 + 2)
                for h in range(P // width):
                    at = slice(h * width, (h + 1) * width)
                    mm = pool.memset(head_blocks[layer][at, at], 1.0)
                    mm = pool.memset(att[at, :, P + h:P + h + 1], 1.0)
                mm.then_inc(att_ones_ready, 1)
                pool.wait_ge(bias_ready, 3 * (layer + 1))
                pool.wait_ge(att_ones_ready, 2 * layer * 2 + 3)
                pool.tensor_tensor(v_bias_blocks[:, :, :], bias_rows[:, V, :].rearrange("p (g n) -> p g n", g=CHUNKS),
                                   head_blocks[layer][:, :].unsqueeze(1).to_broadcast([P, CHUNKS, P]), ALU.mult)\
                    .then_inc(att_ones_ready, 1)
                if layer == 0:
                    pool.wait_ge(masks_step, 7)
                    scale_of(x_moments, x_var, x_rstd, x_moments_done, x_scale_done, 0)

            def bias_residual(j):
                pool.wait_ge(res_loaded, 16 * (j + 1))
                for t in range(TILES):
                    pool.tensor_tensor(x_res[:, t, :], x_res[:, t, :], bias_rows[:, O, :], ALU.add)\
                        .then_inc(res_biased, 1)

            def output_stage(layer, j):
                bias_residual(j)

            def iteration(layer, i, with_output, with_next):
                width = DIM // HEADS[layer]
                if not (isinstance(i, int) and i == 0):
                    pool.wait_ge(att_done, i)
                for n, table in enumerate((sum_mask, v_mask)):
                    row = table[:, bass.ds(i, 1), :].rearrange("p a t -> p (a t)")
                    pool.tensor_copy(v[:, :, :, P + n], row.unsqueeze(2).to_broadcast([P, TILES, CHUNKS]))\
                        .then_inc(v_masks_ready, 1)
                if with_next:
                    scale_of(x_moments, x_var, x_rstd, x_moments_done, x_scale_done, i + 1)
                if with_output:
                    bias_residual(i - 1)
                for t in range(TILES):
                    pool.wait_ge(q_max_done, TILES * i + t + 1)
                    rows_q = q[:, t, :].rearrange("p (h e) -> p h e", e=width)
                    pool.tensor_tensor(rows_q, rows_q, q_max[:, t, 0:HEADS[layer]].unsqueeze(2)
                                       .to_broadcast([P, HEADS[layer], width]), ALU.subtract).then_inc(q_shifted, 1)
                scale_of(y_moments, y_var, y_rstd, y_moments_done, y_scale_done, i)

            run_layers(pool, start_layer, iteration, output_stage)


NAMES = ({Q: "Wq", K: "Wk", V: "Wv", O: "film_out_W"}, {Q: "Wq", K: "Wk", V: "Wv", O: "W_out"})
BIAS_NAMES = ({Q: "bq", K: "bk", V: "bv", O: "film_out_b"}, {Q: "bq", K: "bk", V: "bv", O: "b_out"})
PARAM_NAMES = (
    ("L0_cond_norm_scale", "L0_cond_norm_bias", "L0_cond_bk", "L0_cond_film_norm_scale", "L0_cond_film_norm_bias"),
    ("L1_cond_ln_w", "L1_cond_ln_b", "L1_cond_bk", "L1_cond_ln2_w", "L1_cond_ln2_b"),
)


def kernel(**inputs):
    import numpy as np
    import concourse.bacc as bacc
    from concourse.bass_utils import run_bass_kernel_spmd

    nc = bacc.Bacc("TRN2", target_bir_lowering=False, num_devices=1)
    arrays, aps = {}, {}
    for name, value in inputs.items():
        value = np.ascontiguousarray(value)
        arrays[f"in_{name}"] = value
        aps[name] = nc.dram_tensor(f"in_{name}", value.shape, mybir.dt.from_np(value.dtype),
                                   kind="ExternalInput").ap()
    out = nc.dram_tensor("out_x", (BATCHES, SEQ, DIM), F32, kind="ExternalOutput").ap()
    build_program(nc, aps, out)
    result = run_bass_kernel_spmd(nc, [arrays], core_ids=[0])
    return result.results[0]["out_x"]
```

```python
from contextlib import ExitStack

import concourse.bass as bass
from concourse import mybir

F32 = mybir.dt.float32
F32R = mybir.dt.float32r
I32 = mybir.dt.int32
ALU = mybir.AluOpType
ACT = mybir.ActivationFunctionType
AX_X = mybir.AxisListType.X

P = 128
BATCHES, SEQ, DIM, EMB = 8, 512, 512, 1024
TILES = SEQ // P
CHUNKS = DIM // P
EMB_CHUNKS = EMB // P
LAYERS = 2
HEADS = (16, 8)
ITERS = LAYERS * BATCHES
EPS = 1e-5
MASKED_0 = -1e30
MASKED_1 = -1e6
Q, K, V, O = range(4)
RAW_ORDER = (K, V, Q, O)
VCOLS = P + 2
BCOLS = P + 4
GROUP = 256

PARAMS = 5 * CHUNKS + 2 * CHUNKS
LN_SCALE, LN_BIAS, BK, FILM_SCALE, FILM_BIAS, FILM_EMB_BIAS = (r * CHUNKS for r in range(6))


def build_program(nc, a, out):
    with ExitStack() as ctx:
        def sb(name, shape, dt=F32):
            return ctx.enter_context(nc.sbuf_tensor(name, shape, dt))

        def sem(name):
            return ctx.enter_context(nc.semaphore(name))

        x_mid = nc.dram_tensor("x_between_layers", [BATCHES, SEQ, DIM], F32).ap()

        def rows(ap, b):
            return ap[b, :, :].rearrange("(p t) d -> p t d", t=TILES) if isinstance(b, int) else \
                ap[bass.ds(b, 1), :, :].rearrange("a (p t) d -> (a p) t d", t=TILES)

        source = (a["x"], x_mid)
        target = (x_mid, out)

        w_high = [sb(f"w_high_{n}", [P, CHUNKS, DIM], F32R) for n in "qkvo"]
        w_low = [sb(f"w_low_{n}", [P, CHUNKS, DIM], F32R) for n in "qkvo"]
        raw = sb("raw_weights", [P, 2 * CHUNKS, DIM])
        bias_q = sb("bias_q", [P, DIM])
        bias_v = sb("bias_v", [P, CHUNKS, P])
        bias_o = sb("bias_o", [P, DIM])
        param_in = sb("param_in", [LAYERS * PARAMS, P])
        params = sb("params", [P, LAYERS, PARAMS])
        ident = sb("ident", [P, P])
        ones = sb("ones", [P, P], F32R)
        head_blocks = [sb(f"head_blocks_{n}", [P, P]) for n in range(LAYERS)]
        minus_half = sb("minus_half", [P, TILES])
        masked_in = sb("masked_in", [P, BATCHES, TILES], I32)
        k_mask = sb("k_mask", [P, ITERS, TILES])
        v_mask = sb("v_mask", [P, ITERS, TILES])
        sum_mask = sb("sum_mask", [P, ITERS, TILES])
        film_scale = sb("film_scale", [P, ITERS, CHUNKS])
        film_shift = sb("film_shift", [P, ITERS, CHUNKS])

        x_in = sb("x_in", [P, TILES, DIM])
        x_res = sb("x_res", [P, TILES, DIM])
        x_stats = sb("x_stats", [P, TILES, 6])
        x_moments = sb("x_moments", [P, TILES, 2])
        x_var = sb("x_var", [P, TILES])
        x_rstd = sb("x_rstd", [P, TILES])
        xT = sb("xT", [P, 2, SEQ])
        xT_high = sb("xT_high", [P, CHUNKS, SEQ], F32R)
        xT_low = sb("xT_low", [P, CHUNKS, SEQ], F32R)
        k_max = sb("k_max", [P, DIM])
        k_top = sb("k_top", [P, 3, CHUNKS])
        k_shift = sb("k_shift", [P, CHUNKS, P], F32R)
        k_exp = sb("k_exp", [P, TILES, DIM])
        v = sb("v", [P, TILES, CHUNKS, VCOLS])
        q = sb("q", [P, TILES, DIM])
        q_max = sb("q_max", [P, TILES, HEADS[0]])
        qT = sb("qT", [P, TILES, CHUNKS, P])
        att_sums = sb("att_sums", [P, CHUNKS, 2])
        att_scale = sb("att_scale", [P, 2, CHUNKS])
        att_of = [sb(f"att_{n}", [P, CHUNKS, BCOLS]) for n in range(LAYERS)]
        q_rsum = sb("q_rsum", [P, TILES, HEADS[0]])
        y = sb("y", [P, TILES, DIM])
        y_stats = sb("y_stats", [P, TILES, 6])
        y_moments = sb("y_moments", [P, TILES, 2])
        y_var = sb("y_var", [P, TILES])
        y_rstd = sb("y_rstd", [P, TILES])
        gate = sb("gate", [P, 2, SEQ])
        gT_high = sb("gT_high", [P, CHUNKS, SEQ], F32R)
        gT_low = sb("gT_low", [P, CHUNKS, SEQ], F32R)

        emb = gate[0:BATCHES, :, :].rearrange("p a n -> p (a n)")
        film_row = emb
        embT = sb("embT", [P, EMB_CHUNKS, BATCHES])

        psum_t = ctx.enter_context(nc.psum_tensor("psum_t", [P, 2, CHUNKS, P], F32))
        psum_w = ctx.enter_context(nc.psum_tensor("psum_w", [P, 2, DIM], F32))
        psum_k = ctx.enter_context(nc.psum_tensor("psum_k", [P, TILES, DIM], F32))
        quads = psum_k[:, :, :].rearrange("p a (b n) -> p (a b) n", n=GROUP)
        att_turned_psum = psum_k[:, 0, :].rearrange("p (g n) -> p g n", n=P)
        att_psum = quads[:, 0:CHUNKS, :]

        def y_psum_of(t):
            at = CHUNKS * (t % 2)
            return quads[:, at:at + CHUNKS, :]

        params_loaded, params_turned, params_ready = sem("params_loaded"), sem("params_turned"), sem("params_ready")
        masks_loaded, consts_step, masks_step = sem("masks_loaded"), sem("consts_step"), sem("masks_step")
        emb_loaded, emb_silu, emb_turned, embT_ready = (
            sem("emb_loaded"), sem("emb_silu"), sem("emb_turned"), sem("embT_ready"))
        film_used, film_copied, film_turned, film_step = (
            sem("film_used"), sem("film_copied"), sem("film_turned"), sem("film_step"))
        raw_loaded = [sem("raw_loaded_0"), sem("raw_loaded_1")]
        bias_q_loaded, bias_v_loaded, bias_v_ready, bias_o_loaded = (
            sem("bias_q_loaded"), sem("bias_v_loaded"), sem("bias_v_ready"), sem("bias_o_loaded"))
        w_high_ready, w_low_ready = sem("w_high_ready"), sem("w_low_ready")
        x_loaded, x_stats_done, x_moments_done, x_scale_done, xn_ready = (
            sem("x_loaded"), sem("x_stats_done"), sem("x_moments_done"), sem("x_scale_done"), sem("xn_ready"))
        xT_psum, xT_ready, xT_high_ready, xT_low_ready = (
            sem("xT_psum"), sem("xT_ready"), sem("xT_high_ready"), sem("xT_low_ready"))
        k_psum, k_max_done, k_max_turned, k_top_step, k_shift_ready, k_shifted, k_exp_ready = (
            sem("k_psum"), sem("k_max_done"), sem("k_max_turned"), sem("k_top_step"),
            sem("k_shift_ready"), sem("k_shifted"), sem("k_exp_ready"))
        v_psum, v_ready, v_masks_ready = sem("v_psum"), sem("v_ready"), sem("v_masks_ready")
        q_psum, q_biased, q_max_done, q_shifted, q_exp_ready = (
            sem("q_psum"), sem("q_biased"), sem("q_max_done"), sem("q_shifted"), sem("q_exp_ready"))
        att_done, att_step, att_built, att_turned, att_ready = (
            sem("att_done"), sem("att_step"), sem("att_built"), sem("att_turned"), sem("att_ready"))
        qT_psum, qT_ready = sem("qT_psum"), sem("qT_ready")
        y_psum, q_rsum_done, y_ready, y_stats_done, y_moments_done, y_scale_done, yn_ready = (
            sem("y_psum"), sem("q_rsum_done"), sem("y_ready"), sem("y_stats_done"),
            sem("y_moments_done"), sem("y_scale_done"), sem("yn_ready"))
        yT_psum, gate_ready, g_high_ready, g_low_ready = (
            sem("yT_psum"), sem("gate_ready"), sem("g_high_ready"), sem("g_low_ready"))
        o_psum, res_loaded, res_biased, o_added, stored = (
            sem("o_psum"), sem("res_loaded"), sem("res_biased"), sem("o_added"), sem("stored"))

        minus_half_ready, head_blocks_ready = sem("minus_half_ready"), sem("head_blocks_ready")
        waits_passed = sem("waits_passed")
        MASK_STEPS = 6
        HEAD_BLOCK_PIECES = sum(2 + 2 * (h // CHUNKS) for h in HEADS)
        ATT_STEPS = 3 + CHUNKS
        FILM_STEPS = 5
        RAW_FILM, RAW_LAYER = 4, (0, 4 + 4 * LAYERS)

        block = ctx.enter_context(nc.Block())

        def wait_apart(eng, semaphore, value):
            eng.wait_ge(semaphore, value)
            eng.sem_inc(waits_passed, 1)

        def run_iterations(eng, iteration, output_stage):
            for layer in range(LAYERS):
                first, last = layer * BATCHES, layer * BATCHES + BATCHES - 1
                iteration(layer, first, first > 0, True)
                with eng.Fori(first + 1, last) as i:
                    iteration(layer, i, True, True)
                iteration(layer, last, True, last + 1 < ITERS)
            output_stage(LAYERS - 1, ITERS - 1)

        def fixed(i, value):
            return isinstance(i, int) and i == value

        LAST_0, FIRST_1 = BATCHES - 1, BATCHES

        @block.sync
        def _(sp):
            def key(layer, name):
                return a[("L0_cond_", "L1_cond_")[layer] + name]

            def load_raw(n):
                if n >= 2:
                    free_raw(n - 2)
                if RAW_FILM <= n < RAW_LAYER[1]:
                    layer, part = (n - RAW_FILM) // 4, (n - RAW_FILM) % 4
                    half, k_half = part // 2, part % 2
                    weights = key(layer, ("film_emb_W", "W_emb")[layer])[
                        k_half * EMB // 2:(k_half + 1) * EMB // 2, half * DIM:(half + 1) * DIM]
                else:
                    layer = int(n >= RAW_LAYER[1])
                    weights = key(layer, NAMES[layer][RAW_ORDER[n - RAW_LAYER[layer]]])
                sp.dma_start(raw[:, n % 2 * CHUNKS:(n % 2 + 1) * CHUNKS, :],
                             weights.rearrange("(c p) n -> p c n", p=P)).then_inc(raw_loaded[n % 2], 16)

            def free_raw(n):
                if RAW_FILM <= n < RAW_LAYER[1]:
                    sp.wait_ge(film_used, n - RAW_FILM + 1)
                else:
                    sp.wait_ge(w_low_ready, CHUNKS * (n + 1 if n < RAW_FILM else n + 1 - 4 * LAYERS))

            def load_x(i, layer):
                if layer:
                    sp.wait_ge(stored, 16 * (i - BATCHES + 1))
                sp.dma_start(x_in[:, :, :], rows(source[layer], i - BATCHES * layer)).then_inc(x_loaded, 16)

            def load_bias(layer, m, to, loaded):
                sp.dma_start(to, key(layer, BIAS_NAMES[layer][m]).partition_broadcast(P)).then_inc(loaded, 16)

            bias_v_row = bias_v[:, :, :].rearrange("p g n -> p (g n)")
            load_x(0, 0)
            load_raw(0)
            for layer in range(LAYERS):
                at = layer * PARAMS
                for name in PARAM_NAMES[layer]:
                    n = a[name].shape[0] // P
                    sp.dma_start(param_in[at:at + n, :], a[name].rearrange("(c p) -> c p", p=P))\
                      .then_inc(params_loaded, 16)
                    at += n
            sp.dma_start(emb, a["cond_2048"]).then_inc(emb_loaded, 16)
            sp.dma_start(masked_in[:, :, :], a["mask_BxS_ik0"].rearrange("b (p t) -> p b t", t=TILES))\
              .then_inc(masks_loaded, 16)
            sp.dma_start(v_mask[:, BATCHES:ITERS, :],
                         a["mask_BxSx1_fk1"].rearrange("b (p t) o -> p b (t o)", t=TILES)).then_inc(masks_loaded, 16)
            load_raw(1)
            load_bias(0, Q, bias_q[:, :], bias_q_loaded)
            load_bias(0, V, bias_v_row, bias_v_loaded)
            load_bias(0, O, bias_o[:, :], bias_o_loaded)
            load_raw(2)
            load_raw(3)

            def iteration(layer, i, with_output, with_next):
                if with_next:
                    sp.wait_ge(xT_psum, CHUNKS * (i + 1))
                    load_x(i + 1, 1 if fixed(i, LAST_0) else layer)
                if fixed(i, 0):
                    for n in range(RAW_FILM, RAW_LAYER[1] + 2):
                        load_raw(n)
                if with_output:
                    output_stage(0 if fixed(i, FIRST_1) else layer, i - 1)
                if fixed(i, LAST_0):
                    load_raw(RAW_LAYER[1] + 2)
                    sp.wait_ge(q_biased, TILES * BATCHES)
                    load_bias(1, Q, bias_q[:, :], bias_q_loaded)
                    load_raw(RAW_LAYER[1] + 3)
                    sp.wait_ge(att_built, BATCHES)
                    load_bias(1, V, bias_v_row, bias_v_loaded)
                if fixed(i, FIRST_1):
                    sp.wait_ge(res_biased, TILES * BATCHES)
                    load_bias(1, O, bias_o[:, :], bias_o_loaded)

            def output_stage(layer, j):
                sp.dma_start(x_res[:, :, :], rows(source[layer], j - BATCHES * layer)).then_inc(res_loaded, 16)
                sp.wait_ge(o_added, TILES * (j + 1))
                sp.dma_start(rows(target[layer], j - BATCHES * layer), x_res[:, :, :]).then_inc(stored, 16)
                wait_apart(sp, stored, 16 * (j + 1))

            run_iterations(sp, iteration, output_stage)
            sp.wait_ge(stored, 16 * ITERS)

        @block.tensor
        def _(pe):
            def split_product(dst, lhs_high, lhs_low, rhs_high, rhs_low, before=None):
                for c in range(CHUNKS):
                    if before is not None:
                        before(c)
                    for n, (lhs, rhs) in enumerate(((lhs_high, rhs_high), (lhs_high, rhs_low), (lhs_low, rhs_high))):
                        last = pe.matmul(dst, lhs(c), rhs[:, c, :], start=(c == 0 and n == 0),
                                         stop=(c == CHUNKS - 1 and n == 2))
                return last

            def project(dst, t, m, before=None):
                return split_product(dst, lambda c: xT_high[:, c, t * P:(t + 1) * P],
                                     lambda c: xT_low[:, c, t * P:(t + 1) * P], w_high[m], w_low[m], before)

            def weights_split(layer, n):
                pe.wait_ge(w_high_ready, CHUNKS * (4 * layer + n + 1))
                pe.wait_ge(w_low_ready, CHUNKS * (4 * layer + n + 1))

            def film():
                for n in range(4 * LAYERS):
                    layer, half, k_half = n // 4, n // 2 % 2, n % 2
                    pe.wait_ge(raw_loaded[n % 2], 16 * ((RAW_FILM + n) // 2 + 1))
                    if k_half == 0:
                        if n < 4:
                            pe.wait_ge(q_biased, 3 + half)
                        else:
                            pe.wait_ge(film_copied, half + 1)
                    for c in range(CHUNKS):
                        mm = pe.matmul(psum_w[0:BATCHES, half, :], embT[:, k_half * CHUNKS + c, :],
                                       raw[:, n % 2 * CHUNKS + c, :], start=(k_half == 0 and c == 0),
                                       stop=(k_half == 1 and c == CHUNKS - 1))
                    mm.then_inc(film_used, 1)
                    if n % 4 == 3:
                        pe.wait_ge(film_copied, 2 * layer + 2)
                        if layer:
                            pe.wait_ge(film_step, FILM_STEPS * layer)
                        else:
                            pe.wait_ge(k_top_step, 1)
                        for c in range(2 * CHUNKS):
                            mm = pe.transpose(psum_t[:, 0, 0, c * BATCHES:(c + 1) * BATCHES],
                                              film_row[:, c * P:(c + 1) * P], ident[0:BATCHES, 0:BATCHES])
                        mm.then_inc(film_turned, 1)
                pe.wait_ge(film_step, FILM_STEPS * LAYERS)

            def turn_x(i, c):
                if c == 0:
                    pe.wait_ge(xn_ready, TILES * (i + 1))
                if c >= 2:
                    pe.wait_ge(xT_ready, CHUNKS * i + c - 1)
                elif fixed(i, 0):
                    pe.wait_ge(embT_ready, 1)
                else:
                    pe.wait_ge(qT_ready, TILES * (i - 1) + c + 3)
                for t in range(TILES):
                    mm = pe.transpose(psum_t[:, c % 2, t, :], x_in[:, t, c * P:(c + 1) * P], ident[:, :])
                mm.then_inc(xT_psum, 1)

            def turn_y(j, c):
                if c == 0:
                    pe.wait_ge(yn_ready, TILES * (j + 1))
                if c < 2:
                    pe.wait_ge(xT_ready, CHUNKS * (min(j + 2, ITERS) if isinstance(j, int) else j + 2) - 1 + c)
                else:
                    pe.wait_ge(gate_ready, CHUNKS * j + c - 1)
                for t in range(TILES):
                    mm = pe.transpose(psum_t[:, c % 2, t, :], y[:, t, c * P:(c + 1) * P], ident[:, :])
                mm.then_inc(yT_psum, 1)

            def out_projection(j, t, alone=False):
                if t == 0:
                    pe.wait_ge(g_low_ready, CHUNKS * (j + 1))
                if t >= 2:
                    pe.wait_ge(o_added, TILES * j + t - 1)
                elif alone:
                    pe.wait_ge(q_biased, TILES * (j + 1))
                else:
                    pe.wait_ge(q_biased, TILES * (j + 1) + t + 3)
                split_product(psum_w[:, t % 2, :], lambda c: gT_high[:, c, t * P:(t + 1) * P],
                              lambda c: gT_low[:, c, t * P:(t + 1) * P], w_high[O], w_low[O]).then_inc(o_psum, 1)

            def output_stage(layer, j):
                for c in range(CHUNKS):
                    turn_y(j, c)
                for t in range(TILES):
                    out_projection(j, t, alone=True)

            pe.wait_ge(params_loaded, 16 * 6 * LAYERS)
            pe.wait_ge(consts_step, 3)
            pe.transpose(psum_t[:, 0, 0, 0:LAYERS * PARAMS], param_in[:, :],
                         ident[0:LAYERS * PARAMS, 0:LAYERS * PARAMS]).then_inc(params_turned, 1)
            pe.wait_ge(emb_silu, 1)
            for c in range(EMB_CHUNKS):
                mm = pe.transpose(psum_t[:, 1, 0, c * BATCHES:(c + 1) * BATCHES],
                                  emb[:, c * P:(c + 1) * P], ident[0:BATCHES, 0:BATCHES])
            mm.then_inc(emb_turned, 1)
            pe.wait_ge(params_ready, 1)
            for c in range(CHUNKS):
                turn_x(0, c)

            def iteration(layer, i, with_output, with_next):
                def k_ready(c):
                    pe.wait_ge(xT_low_ready, CHUNKS * i + c + 1)

                if fixed(i, layer * BATCHES):
                    weights_split(layer, 0)
                for t in range(TILES):
                    if not fixed(i, 0):
                        if t == 0:
                            pe.wait_ge(y_ready, TILES * (i - 1) + 3)
                        if t == 2:
                            pe.wait_ge(y_ready, TILES * i)
                    project(psum_k[:, t, :], t, K, k_ready if t == 0 else None).then_inc(k_psum, 1)

                def v_projection(t):
                    if t >= 2:
                        pe.wait_ge(v_ready, TILES * i + t - 1)
                    project(psum_w[:, t % 2, :], t, V).then_inc(v_psum, 1)

                if fixed(i, layer * BATCHES):
                    weights_split(layer, 1)
                if with_output:
                    turn_y(i - 1, 0)
                    turn_y(i - 1, 1)
                v_projection(0)
                if with_output:
                    turn_y(i - 1, 2)
                    turn_y(i - 1, 3)
                v_projection(1)
                pe.wait_ge(k_max_done, TILES * (i + 1))
                if with_output:
                    pe.wait_ge(gate_ready, CHUNKS * (i - 1) + 3)
                else:
                    pe.wait_ge(xT_ready, CHUNKS * i + 3)
                for c in range(CHUNKS):
                    mm = pe.transpose(psum_t[:, 0, c, :], k_max[:, c * P:(c + 1) * P], ident[:, :])
                mm.then_inc(k_max_turned, 1)
                v_projection(2)
                pe.wait_ge(k_shift_ready, i + 1)
                for t in range(TILES):
                    pe.matmul(psum_k[:, t, :], ones[:, :], k_shift[:, :, :].rearrange("p c n -> p (c n)"),
                              start=False, stop=True, skip_group_check=True).then_inc(k_shifted, 1)
                v_projection(3)
                if fixed(i, layer * BATCHES):
                    weights_split(layer, 2)
                for t in range(TILES):
                    if t < 2:
                        pe.wait_ge(v_ready, TILES * i + t + 3)
                    else:
                        pe.wait_ge(q_biased, TILES * i + t - 1)
                    project(psum_w[:, t % 2, :], t, Q).then_inc(q_psum, 1)
                pe.wait_ge(k_exp_ready, TILES * (i + 1))
                pe.wait_ge(v_ready, TILES * (i + 1))
                pe.wait_ge(v_masks_ready, 2 * (i + 1))
                for g in range(CHUNKS):
                    for t in range(TILES):
                        mm = pe.matmul(att_psum[:, g, 0:VCOLS], k_exp[:, t, g * P:(g + 1) * P], v[:, t, g, :],
                                       start=(t == 0), stop=(t == TILES - 1))
                mm.then_inc(att_done, 1)

                def turn_att():
                    pe.wait_ge(att_built, i + 1)
                    for g in range(CHUNKS):
                        mm = pe.transpose(att_turned_psum[:, g, :], att_of[layer][:, g, 0:P], ident[:, :])
                    mm.then_inc(att_turned, 1)

                def turn_q(t):
                    pe.wait_ge(q_exp_ready, TILES * i + t + 1)
                    if t == 0:
                        pe.wait_ge(k_top_step, 3 * i + 1)
                    elif t == 1:
                        if with_output:
                            pe.wait_ge(gate_ready, CHUNKS * i)
                        else:
                            pe.wait_ge(xT_ready, CHUNKS * i + 4)
                    else:
                        pe.wait_ge(qT_ready, TILES * i + t - 1)
                    for c in range(CHUNKS):
                        mm = pe.transpose(psum_t[:, t % 2, c, :], q[:, t, c * P:(c + 1) * P], ident[:, :])
                    mm.then_inc(qT_psum, 1)

                def attend(t):
                    pe.wait_ge(qT_ready, TILES * i + t + 1)
                    if t == 0:
                        pe.wait_ge(att_ready, i + 1)
                    if t >= 2:
                        pe.wait_ge(y_ready, TILES * i + t - 1)
                    for g in range(CHUNKS):
                        mm = pe.matmul(y_psum_of(t)[:, g, 0:BCOLS], qT[:, t, g, :], att_of[layer][:, g, :],
                                       start=True, stop=True)
                    mm.then_inc(y_psum, 1)

                if fixed(i, 0):
                    film()
                if with_output:
                    out_projection(i - 1, 0)
                    out_projection(i - 1, 1)
                if layer == 0:
                    turn_att()
                turn_q(0)
                turn_q(1)
                if with_output:
                    out_projection(i - 1, 2)
                turn_q(2)
                turn_q(3)
                if with_output:
                    out_projection(i - 1, 3)
                if fixed(i, 0):
                    weights_split(0, 3)
                if fixed(i, FIRST_1):
                    weights_split(1, 3)
                if with_next:
                    turn_x(i + 1, 0)
                    turn_x(i + 1, 1)
                attend(0)
                attend(1)
                if with_next:
                    turn_x(i + 1, 2)
                    turn_x(i + 1, 3)
                attend(2)
                attend(3)

            run_iterations(pe, iteration, output_stage)

        @block.vector
        def _(dve):
            def next_x(i):
                dve.wait_ge(x_loaded, 16 * (i + 1))
                for t in range(TILES):
                    dve.bn_stats(x_stats[:, t, :], x_in[:, t, :]).then_inc(x_stats_done, 1)
                for t in range(TILES):
                    wait_apart(dve, x_stats_done, TILES * i + t + 1)
                    dve.bn_aggr(x_moments[:, t, :], x_stats[:, t, :]).then_inc(x_moments_done, 1)

            def next_xn(i):
                dve.wait_ge(x_scale_done, 2 * (i + 1))
                dve.wait_ge(x_moments_done, TILES * (i + 1))
                for t in range(TILES):
                    dve.tensor_scalar(x_in[:, t, :], x_in[:, t, :], x_moments[:, t, 0:1], x_rstd[:, t:t + 1],
                                      ALU.subtract, ALU.mult).then_inc(xn_ready, 1)

            def split_weights(layer, n):
                m, slot = RAW_ORDER[n], (RAW_LAYER[layer] + n) % 2
                for c in range(CHUNKS):
                    dve.wait_ge(w_high_ready, CHUNKS * (4 * layer + n) + c + 1)
                    dve.tensor_tensor(w_low[m][:, c, :], raw[:, slot * CHUNKS + c, :], w_high[m][:, c, :],
                                      ALU.subtract).then_inc(w_low_ready, 1)

            def split_x(i, c):
                dve.wait_ge(xT_high_ready, CHUNKS * i + c + 1)
                dve.tensor_tensor(xT_low[:, c, :], xT[:, c % 2, :], xT_high[:, c, :], ALU.subtract)\
                   .then_inc(xT_low_ready, 1)

            def v_bias_blocks(layer):
                dve.wait_ge(bias_v_loaded, 16 * (layer + 1))
                dve.wait_ge(head_blocks_ready, HEAD_BLOCK_PIECES)
                dve.tensor_tensor(bias_v[:, :, :], bias_v[:, :, :],
                                  head_blocks[layer][:, :].unsqueeze(1).to_broadcast([P, CHUNKS, P]), ALU.mult)\
                   .then_inc(bias_v_ready, 1)

            dve.memset(minus_half[:, :], -0.5).then_inc(minus_half_ready, 1)
            next_x(0)
            dve.wait_ge(params_turned, 1)
            dve.tensor_copy(params[:, :, :].rearrange("p l r -> p (l r)"),
                            psum_t[:, 0, 0, 0:LAYERS * PARAMS]).then_inc(params_ready, 1)
            dve.wait_ge(emb_turned, 1)
            dve.tensor_copy(embT[:, :, :].rearrange("p c b -> p (c b)"),
                            psum_t[:, 1, 0, 0:EMB_CHUNKS * BATCHES]).then_inc(embT_ready, 1)
            next_xn(0)
            split_weights(0, 0)
            for c in range(CHUNKS):
                split_x(0, c)
            dve.wait_ge(masks_loaded, 32)
            m0, m1 = slice(0, BATCHES), slice(BATCHES, ITERS)
            dve.memset(sum_mask[:, m1, :], 1.0).then_inc(masks_step, 1)
            dve.tensor_scalar(k_mask[:, m0, :], masked_in[:, :, :], 1.0, MASKED_0,
                              ALU.is_equal, ALU.mult).then_inc(masks_step, 1)
            dve.tensor_scalar(v_mask[:, m0, :], masked_in[:, :, :], 1.0, None, ALU.not_equal).then_inc(masks_step, 1)
            dve.tensor_scalar(sum_mask[:, m0, :], masked_in[:, :, :], 1.0, None, ALU.not_equal).then_inc(masks_step, 1)
            dve.tensor_scalar(k_mask[:, m1, :], v_mask[:, m1, :], -1.0, 1.0, ALU.mult, ALU.add).then_inc(masks_step, 1)
            dve.wait_ge(masks_step, 5)
            dve.tensor_scalar(k_mask[:, m1, :], k_mask[:, m1, :], MASKED_1, None, ALU.mult).then_inc(masks_step, 1)
            dve.wait_ge(masks_step, MASK_STEPS)
            split_weights(0, 1)

            def film():
                for n in range(2 * LAYERS):
                    layer, half = n // 2, n % 2
                    dve.wait_ge(film_used, 2 * (n + 1))
                    if n == 2:
                        dve.wait_ge(film_turned, 1)
                    dve.tensor_copy(film_row[:, half * DIM:(half + 1) * DIM], psum_w[0:BATCHES, half, :])\
                       .then_inc(film_copied, 1)
                    if half:
                        at = slice(layer * BATCHES, (layer + 1) * BATCHES)
                        scale = film_scale[:, at, :].rearrange("p b c -> p c b")
                        shift = film_shift[:, at, :].rearrange("p b c -> p c b")
                        cols = psum_t[:, 0, 0, 0:2 * CHUNKS * BATCHES].rearrange("p (h c b) -> p h c b", h=2, b=BATCHES)

                        def param(r):
                            return params[:, layer, r:r + CHUNKS].unsqueeze(2).to_broadcast([P, CHUNKS, BATCHES])

                        at = FILM_STEPS * layer
                        dve.wait_ge(film_turned, layer + 1)
                        dve.tensor_tensor(scale, cols[:, 0], param(FILM_EMB_BIAS), ALU.add).then_inc(film_step, 1)
                        dve.wait_ge(film_step, at + 1)
                        dve.scalar_tensor_tensor(out=shift, in0=scale, scalar=1.0, in1=param(FILM_BIAS),
                                                 op0=ALU.add, op1=ALU.mult).then_inc(film_step, 1)
                        dve.wait_ge(film_step, at + 2)
                        dve.scalar_tensor_tensor(out=scale, in0=scale, scalar=1.0, in1=param(FILM_SCALE),
                                                 op0=ALU.add, op1=ALU.mult).then_inc(film_step, 1)
                        dve.tensor_tensor(shift, shift, cols[:, 1], ALU.add).then_inc(film_step, 1)
                        dve.wait_ge(film_step, at + 4)
                        dve.tensor_tensor(shift, shift, param(FILM_EMB_BIAS + CHUNKS), ALU.add).then_inc(film_step, 1)

            def normalise_y(j):
                dve.wait_ge(y_scale_done, 2 * (j + 1))
                dve.wait_ge(y_moments_done, TILES * (j + 1))
                for t in range(TILES):
                    dve.tensor_scalar(y[:, t, :], y[:, t, :], y_moments[:, t, 0:1], y_rstd[:, t:t + 1],
                                      ALU.subtract, ALU.mult).then_inc(yn_ready, 1)

            def split_gate(j, c):
                dve.wait_ge(g_high_ready, CHUNKS * j + c + 1)
                dve.tensor_tensor(gT_low[:, c, :], gate[:, c % 2, :], gT_high[:, c, :], ALU.subtract)\
                   .then_inc(g_low_ready, 1)

            def add_residual(j, t):
                dve.wait_ge(o_psum, TILES * j + t + 1)
                dve.wait_ge(res_biased, TILES * j + t + 1)
                dve.tensor_tensor(x_res[:, t, :], x_res[:, t, :], psum_w[:, t % 2, :], ALU.add).then_inc(o_added, 1)

            def output_stage(layer, j):
                normalise_y(j)
                for c in range(CHUNKS):
                    split_gate(j, c)
                for t in range(TILES):
                    add_residual(j, t)

            def iteration(layer, i, with_output, with_next):
                heads = HEADS[layer]
                per_group = heads // CHUNKS
                width = DIM // heads
                att = att_of[layer]
                if with_output:
                    normalise_y(i - 1)
                for t in range(TILES):
                    dve.wait_ge(k_psum, TILES * i + t + 1)
                    mask = k_mask[:, bass.ds(i, 1), t:t + 1].rearrange("p a t -> p (a t)")
                    if t == 0:
                        dve.tensor_scalar(k_max[:, :], psum_k[:, t, :], mask, None, ALU.add).then_inc(k_max_done, 1)
                    else:
                        dve.wait_ge(k_max_done, TILES * i + t)
                        dve.scalar_tensor_tensor(out=k_max[:, :], in0=psum_k[:, t, :], scalar=mask,
                                                 in1=k_max[:, :], op0=ALU.add, op1=ALU.max).then_inc(k_max_done, 1)
                if with_output:
                    for c in range(CHUNKS):
                        split_gate(i - 1, c)
                dve.wait_ge(k_max_turned, i + 1)
                dve.tensor_reduce(k_top[:, 0, :], psum_t[:, 0, :, :], AX_X, ALU.max).then_inc(k_top_step, 1)
                dve.wait_ge(k_top_step, 3 * i + 1)
                dve.tensor_tensor(k_top[:, 1, :], k_top[:, 0, :], params[:, layer, BK:BK + CHUNKS], ALU.add).then_inc(k_top_step, 1)
                dve.wait_ge(k_top_step, 3 * i + 2)
                dve.tensor_tensor(k_top[:, 2, :], params[:, layer, BK:BK + CHUNKS], k_top[:, 1, :], ALU.subtract).then_inc(k_top_step, 1)
                dve.wait_ge(k_top_step, 3 * i + 3)
                dve.tensor_tensor(k_shift[:, :, :], ident[:, :].unsqueeze(1).to_broadcast([P, CHUNKS, P]),
                                  k_top[:, 2, :].unsqueeze(2).to_broadcast([P, CHUNKS, P]), ALU.mult)\
                   .then_inc(k_shift_ready, 1)
                if fixed(i, 0):
                    split_weights(0, 2)
                    v_bias_blocks(0)
                    dve.wait_ge(bias_q_loaded, 16)
                if fixed(i, LAST_0):
                    split_weights(1, 0)
                if fixed(i, FIRST_1):
                    split_weights(1, 2)
                    v_bias_blocks(1)
                    dve.wait_ge(bias_q_loaded, 32)
                if with_next:
                    next_x(i + 1)
                for t in range(TILES):
                    dve.wait_ge(q_psum, TILES * i + t + 1)
                    dve.tensor_tensor(q[:, t, :], psum_w[:, t % 2, :], bias_q[:, :], ALU.add)\
                       .then_inc(q_biased, 1)
                    dve.wait_ge(q_biased, TILES * i + t + 1)
                    dve.tensor_reduce(q_max[:, t, 0:heads], q[:, t, :].rearrange("p (h e) -> p h e", e=width),
                                      AX_X, ALU.max).then_inc(q_max_done, 1)
                if with_next:
                    next_xn(i + 1)
                if fixed(i, 0):
                    split_weights(0, 3)
                dve.wait_ge(att_done, i + 1)
                dve.tensor_copy(att_sums[:, :, :], att_psum[:, :, P:VCOLS]).then_inc(att_step, 1)
                dve.wait_ge(att_step, ATT_STEPS * i + 1)
                dve.reciprocal(att_scale[:, 0, :], att_sums[:, :, 0]).then_inc(att_step, 1)
                dve.wait_ge(att_step, ATT_STEPS * i + 2)
                dve.tensor_tensor(att_scale[:, 1, :], att_scale[:, 0, :], att_sums[:, :, 1], ALU.mult)\
                   .then_inc(att_step, 1)
                for g in range(CHUNKS):
                    dve.scalar_tensor_tensor(out=att[:, g, 0:P], in0=att_psum[:, g, 0:P],
                                             scalar=att_scale[:, 0, g:g + 1], in1=head_blocks[layer][:, :],
                                             op0=ALU.mult, op1=ALU.mult).then_inc(att_step, 1)
                dve.wait_ge(att_step, ATT_STEPS * (i + 1))
                for g in range(CHUNKS):
                    mm = dve.scalar_tensor_tensor(out=att[:, g, 0:P], in0=bias_v[:, g, :],
                                                  scalar=att_scale[:, 1, g:g + 1], in1=att[:, g, 0:P],
                                                  op0=ALU.mult, op1=ALU.add)
                mm.then_inc(att_ready if layer else att_built, 1)
                if fixed(i, 0):
                    film()
                if with_output:
                    add_residual(i - 1, 0)
                    add_residual(i - 1, 1)
                if layer == 0:
                    dve.wait_ge(att_turned, i + 1)
                    dve.tensor_copy(att[:, :, 0:P], att_turned_psum).then_inc(att_ready, 1)
                if with_output:
                    add_residual(i - 1, 2)
                    add_residual(i - 1, 3)
                if fixed(i, LAST_0):
                    split_weights(1, 1)
                if fixed(i, FIRST_1):
                    split_weights(1, 3)
                for t in range(TILES):
                    if with_next:
                        split_x(i + 1, t)
                    ps = y_psum_of(t)
                    rsum = q_rsum[:, t, 0:heads].rearrange("p (g h) -> p g h", g=CHUNKS)
                    dve.wait_ge(y_psum, TILES * i + t + 1)
                    dve.reciprocal(rsum, ps[:, :, P:P + per_group]).then_inc(q_rsum_done, 1)
                    dve.wait_ge(q_rsum_done, TILES * i + t + 1)
                    dve.tensor_tensor(
                        y[:, t, :].rearrange("p (g h e) -> p g h e", g=CHUNKS, h=per_group),
                        ps[:, :, 0:P].rearrange("p g (h e) -> p g h e", h=per_group),
                        rsum.unsqueeze(3).to_broadcast([P, CHUNKS, per_group, width]), ALU.mult).then_inc(y_ready, 1)
                for t in range(TILES):
                    dve.wait_ge(y_ready, TILES * i + t + 1)
                    dve.bn_stats(y_stats[:, t, :], y[:, t, :]).then_inc(y_stats_done, 1)
                for t in range(TILES):
                    wait_apart(dve, y_stats_done, TILES * i + t + 1)
                    dve.bn_aggr(y_moments[:, t, :], y_stats[:, t, :]).then_inc(y_moments_done, 1)

            run_iterations(dve, iteration, output_stage)

        @block.scalar
        def _(act):
            def split_weights(layer, n):
                m, at = RAW_ORDER[n], RAW_LAYER[layer] + n
                act.wait_ge(raw_loaded[at % 2], 16 * (at // 2 + 1))
                if layer:
                    act.wait_ge({K: k_psum, V: v_psum, Q: q_psum, O: o_psum}[m], TILES * BATCHES)
                for c in range(CHUNKS):
                    act.copy(w_high[m][:, c, :], raw[:, at % 2 * CHUNKS + c, :]).then_inc(w_high_ready, 1)

            def scale_x(i, layer):
                for c in range(CHUNKS):
                    act.wait_ge(xT_psum, CHUNKS * i + c + 1)
                    if c >= 2:
                        act.wait_ge(xT_low_ready, CHUNKS * i + c - 1)
                    act.activation(xT[:, c % 2, :], psum_t[:, c % 2, :, :].rearrange("p t s -> p (t s)"),
                                   ACT.Identity, scale=params[:, layer, LN_SCALE + c:LN_SCALE + c + 1],
                                   bias=params[:, layer, LN_BIAS + c:LN_BIAS + c + 1]).then_inc(xT_ready, 1)
                    act.wait_ge(xT_ready, CHUNKS * i + c + 1)
                    act.copy(xT_high[:, c, :], xT[:, c % 2, :]).then_inc(xT_high_ready, 1)

            act.wait_ge(emb_loaded, 16)
            act.activation(emb, emb, ACT.Silu).then_inc(emb_silu, 1)
            split_weights(0, 0)
            act.wait_ge(params_ready, 1)
            scale_x(0, 0)
            split_weights(0, 1)
            split_weights(0, 2)

            def activate(j, c):
                act.wait_ge(yT_psum, CHUNKS * j + c + 1)
                if c >= 2:
                    act.wait_ge(g_low_ready, CHUNKS * j + c - 1)
                cond = bass.ds(j, 1)
                act.activation(gate[:, c % 2, :], psum_t[:, c % 2, :, :].rearrange("p t s -> p (t s)"), ACT.Silu,
                               scale=film_scale[:, cond, c:c + 1].rearrange("p a c -> p (a c)"),
                               bias=film_shift[:, cond, c:c + 1].rearrange("p a c -> p (a c)")).then_inc(gate_ready, 1)
                act.wait_ge(gate_ready, CHUNKS * j + c + 1)
                act.copy(gT_high[:, c, :], gate[:, c % 2, :]).then_inc(g_high_ready, 1)

            def output_stage(layer, j):
                for c in range(CHUNKS):
                    activate(j, c)

            def iteration(layer, i, with_output, with_next):
                if with_output:
                    for c in range(CHUNKS):
                        activate(i - 1, c)

                def mask_v(t):
                    act.wait_ge(v_psum, TILES * i + t + 1)
                    act.activation(v[:, t, :, 0:P], psum_w[:, t % 2, :].rearrange("p (g n) -> p g n", g=CHUNKS),
                                   ACT.Copy, scale=v_mask[:, bass.ds(i, 1), t:t + 1].rearrange("p a t -> p (a t)"))\
                       .then_inc(v_ready, 1)

                if fixed(i, 0):
                    act.wait_ge(masks_step, MASK_STEPS)
                mask_v(0)
                mask_v(1)
                for t in range(TILES):
                    act.wait_ge(k_shifted, TILES * i + t + 1)
                    act.activation(k_exp[:, t, :], psum_k[:, t, :], ACT.Exp,
                                   bias=k_mask[:, bass.ds(i, 1), t:t + 1].rearrange("p a t -> p (a t)"))\
                       .then_inc(k_exp_ready, 1)
                mask_v(2)
                mask_v(3)
                if fixed(i, 0):
                    split_weights(0, 3)
                if fixed(i, LAST_0):
                    split_weights(1, 0)
                if fixed(i, FIRST_1):
                    split_weights(1, 2)
                for t in range(TILES):
                    act.wait_ge(q_shifted, TILES * i + t + 1)
                    act.activation(q[:, t, :], q[:, t, :], ACT.Exp).then_inc(q_exp_ready, 1)
                for t in range(TILES):
                    act.wait_ge(qT_psum, TILES * i + t + 1)
                    act.copy(qT[:, t, :, :], psum_t[:, t % 2, :, :]).then_inc(qT_ready, 1)
                    if t == 1 and fixed(i, LAST_0):
                        split_weights(1, 1)
                if fixed(i, FIRST_1):
                    split_weights(1, 3)
                if with_next:
                    scale_x(i + 1, 1 if fixed(i, LAST_0) else layer)

            run_iterations(act, iteration, output_stage)

        @block.gpsimd
        def _(pool):
            def scale_of(moments, var, rstd, count, done, i):
                wait_apart(pool, count, TILES * (i + 1))
                pool.tensor_scalar(var[:, :], moments[:, :, 1], EPS, None, ALU.add).then_inc(done, 1)
                pool.wait_ge(done, 2 * i + 1)
                pool.tensor_tensor(rstd[:, :], var[:, :], minus_half[:, :], ALU.pow).then_inc(done, 1)

            pool.memset(ident[:, :], 0.0).then_inc(consts_step, 1)
            pool.memset(ones[:, :].bitcast(F32), 1.0).then_inc(consts_step, 1)
            pool.wait_ge(consts_step, 2)
            pool.affine_select(out=ident[:, :], in_=ident[:, :], compare_op=ALU.not_equal, fill=1.0,
                               base=0, pattern=[[-1, P]], channel_multiplier=1).then_inc(consts_step, 1)
            pool.wait_ge(minus_half_ready, 1)
            scale_of(x_moments, x_var, x_rstd, x_moments_done, x_scale_done, 0)
            pieces = 0
            for layer in range(LAYERS):
                width = DIM // HEADS[layer]
                steps = [(head_blocks[layer][:, :], 0.0), (att_of[layer][:, :, :], 0.0)]
                for h in range(P // width):
                    at = slice(h * width, (h + 1) * width)
                    steps += [(att_of[layer][at, :, P + h:P + h + 1], 1.0), (head_blocks[layer][at, at], 1.0)]
                for piece, value in steps:
                    pool.memset(piece, value).then_inc(head_blocks_ready, 1)
                    pieces += 1
                    pool.wait_ge(head_blocks_ready, pieces)
            pool.wait_ge(masks_step, MASK_STEPS)
            pool.wait_ge(bias_o_loaded, 16)

            def bias_residual(j):
                pool.wait_ge(res_loaded, 16 * (j + 1))
                for t in range(TILES):
                    pool.tensor_tensor(x_res[:, t, :], x_res[:, t, :], bias_o[:, :], ALU.add)\
                        .then_inc(res_biased, 1)

            def output_stage(layer, j):
                bias_residual(j)

            def iteration(layer, i, with_output, with_next):
                width = DIM // HEADS[layer]
                if not (isinstance(i, int) and i == 0):
                    pool.wait_ge(att_done, i)
                for n, table in enumerate((sum_mask, v_mask)):
                    row = table[:, bass.ds(i, 1), :].rearrange("p a t -> p (a t)")
                    pool.tensor_copy(v[:, :, :, P + n], row.unsqueeze(2).to_broadcast([P, TILES, CHUNKS]))\
                        .then_inc(v_masks_ready, 1)
                if with_next:
                    scale_of(x_moments, x_var, x_rstd, x_moments_done, x_scale_done, i + 1)
                if with_output:
                    bias_residual(i - 1)
                for t in range(TILES):
                    pool.wait_ge(q_max_done, TILES * i + t + 1)
                    rows_q = q[:, t, :].rearrange("p (h e) -> p h e", e=width)
                    pool.tensor_tensor(rows_q, rows_q, q_max[:, t, 0:HEADS[layer]].unsqueeze(2)
                                       .to_broadcast([P, HEADS[layer], width]), ALU.subtract).then_inc(q_shifted, 1)
                scale_of(y_moments, y_var, y_rstd, y_moments_done, y_scale_done, i)
                if fixed(i, FIRST_1):
                    pool.wait_ge(bias_o_loaded, 32)

            run_iterations(pool, iteration, output_stage)


NAMES = ({Q: "Wq", K: "Wk", V: "Wv", O: "film_out_W"}, {Q: "Wq", K: "Wk", V: "Wv", O: "W_out"})
BIAS_NAMES = ({Q: "bq", K: "bk", V: "bv", O: "film_out_b"}, {Q: "bq", K: "bk", V: "bv", O: "b_out"})
PARAM_NAMES = (
    ("L0_cond_norm_scale", "L0_cond_norm_bias", "L0_cond_bk", "L0_cond_film_norm_scale", "L0_cond_film_norm_bias",
     "L0_cond_film_emb_b"),
    ("L1_cond_ln_w", "L1_cond_ln_b", "L1_cond_bk", "L1_cond_ln2_w", "L1_cond_ln2_b", "L1_cond_b_emb"),
)


def kernel(**inputs):
    import numpy as np
    import concourse.bacc as bacc
    from concourse.bass_utils import run_bass_kernel_spmd

    nc = bacc.Bacc("TRN2", target_bir_lowering=False, num_devices=1)
    arrays, aps = {}, {}
    for name, value in inputs.items():
        value = np.ascontiguousarray(value)
        arrays[f"in_{name}"] = value
        aps[name] = nc.dram_tensor(f"in_{name}", value.shape, mybir.dt.from_np(value.dtype),
                                   kind="ExternalInput").ap()
    out = nc.dram_tensor("out_x", (BATCHES, SEQ, DIM), F32, kind="ExternalOutput").ap()
    build_program(nc, aps, out)
    result = run_bass_kernel_spmd(nc, [arrays], core_ids=[0])
    return result.results[0]["out_x"]
```

```python
from contextlib import ExitStack

import concourse.bass as bass
from concourse import mybir

F32 = mybir.dt.float32
F32R = mybir.dt.float32r
I32 = mybir.dt.int32
ALU = mybir.AluOpType
ACT = mybir.ActivationFunctionType
AX_X = mybir.AxisListType.X

P = 128
BATCHES, SEQ, DIM, EMB = 8, 512, 512, 1024
TILES = SEQ // P
CHUNKS = DIM // P
EMB_CHUNKS = EMB // P
LAYERS = 2
HEADS = (16, 8)
ITERS = LAYERS * BATCHES
EPS = 1e-5
MASKED_0 = -1e30
MASKED_1 = -1e6
Q, K, V, O = range(4)
SPLIT_ORDER = (K, V, Q, O)
FILM_PARTS = 4
RAW_PARTS = ([("weights", 0, m) for m in (K, V, Q)] + [("film", 0, n) for n in range(FILM_PARTS)]
             + [("weights", 0, O)] + [("film", 1, n) for n in range(FILM_PARTS)]
             + [("weights", 1, m) for m in SPLIT_ORDER])
RAW_BEFORE_0, RAW_IN_0, RAW_IN_LAST_0 = 3, 10, 15
FILM_AT = (O, K)
VCOLS = P + 2
BCOLS = P + 4
GROUP = 256

PARAMS = (5 + 2) * CHUNKS
LN_SCALE, LN_BIAS, BK, FILM_SCALE, FILM_BIAS, FILM_EMB_BIAS = (r * CHUNKS for r in range(6))


def build_program(nc, a, out):
    with ExitStack() as ctx:
        def sb(name, shape, dt=F32):
            return ctx.enter_context(nc.sbuf_tensor(name, shape, dt))

        def sem(name):
            return ctx.enter_context(nc.semaphore(name))

        x_mid = nc.dram_tensor("x_between_layers", [BATCHES, SEQ, DIM], F32).ap()

        def rows(ap, b):
            return ap[b, :, :].rearrange("(p t) d -> p t d", t=TILES) if isinstance(b, int) else \
                ap[bass.ds(b, 1), :, :].rearrange("a (p t) d -> (a p) t d", t=TILES)

        source = (a["x"], x_mid)
        target = (x_mid, out)

        w_high = [sb(f"w_high_{n}", [P, CHUNKS, DIM], F32R) for n in "qkvo"]
        w_low = [sb(f"w_low_{n}", [P, CHUNKS, DIM], F32R) for n in "qkvo"]
        raw = sb("raw_weights", [P, 2 * CHUNKS, DIM])
        bias_q = sb("bias_q", [P, DIM])
        bias_v = sb("bias_v", [P, CHUNKS, P])
        bias_o = sb("bias_o", [P, DIM])
        param_in = sb("param_in", [PARAMS, LAYERS, P])
        params = sb("params", [P, LAYERS, PARAMS])
        ident = sb("ident", [P, P])
        ones = sb("ones", [P, P], F32R)
        head_blocks = [sb(f"head_blocks_{n}", [P, P]) for n in range(LAYERS)]
        minus_half = sb("minus_half", [P, TILES])
        table_scratch = sb("table_scratch", [P, 2])
        mask_top = sb("mask_top", [P, BATCHES])
        masked_in = sb("masked_in", [P, BATCHES, TILES], I32)
        k_mask = sb("k_mask", [P, ITERS, TILES])
        v_mask = sb("v_mask", [P, ITERS, TILES])
        sum_mask = sb("sum_mask", [P, ITERS, TILES])
        film_scale = sb("film_scale", [P, ITERS, CHUNKS])
        film_shift = sb("film_shift", [P, ITERS, CHUNKS])

        x_in = sb("x_in", [P, TILES, DIM])
        x_res = sb("x_res", [P, TILES, DIM])
        x_stats = sb("x_stats", [P, TILES, 6])
        x_moments = sb("x_moments", [P, TILES, 2])
        x_var = sb("x_var", [P, TILES])
        x_rstd = sb("x_rstd", [P, TILES])
        xT = sb("xT", [P, 2, SEQ])
        xT_high = sb("xT_high", [P, CHUNKS, SEQ], F32R)
        xT_low = sb("xT_low", [P, CHUNKS, SEQ], F32R)
        k_max = sb("k_max", [P, DIM])
        k_top = sb("k_top", [P, 3, CHUNKS])
        k_shift = sb("k_shift", [P, CHUNKS, P], F32R)
        k_shift_rows = sb("k_shift_rows", [P, DIM])
        k_exp = sb("k_exp", [P, TILES, DIM])
        v = sb("v", [P, TILES, CHUNKS, VCOLS])
        q = sb("q", [P, TILES, DIM])
        q_max = sb("q_max", [P, TILES, HEADS[0]])
        qT = sb("qT", [P, TILES, CHUNKS, P])
        att_sums = sb("att_sums", [P, CHUNKS, 2])
        att_scale = sb("att_scale", [P, 2, CHUNKS])
        att_of = [sb(f"att_{n}", [P, CHUNKS, BCOLS]) for n in range(LAYERS)]
        q_rsum = sb("q_rsum", [P, TILES, HEADS[0]])
        y = sb("y", [P, TILES, DIM])
        y_stats = sb("y_stats", [P, TILES, 6])
        y_moments = sb("y_moments", [P, TILES, 2])
        y_var = sb("y_var", [P, TILES])
        y_rstd = sb("y_rstd", [P, TILES])
        gate = sb("gate", [P, 2, SEQ])
        gT_high = sb("gT_high", [P, CHUNKS, SEQ], F32R)
        gT_low = sb("gT_low", [P, CHUNKS, SEQ], F32R)

        emb = gate[0:BATCHES, :, :].rearrange("p a n -> p (a n)")
        film_rows = gate[0:2 * BATCHES, :, :].rearrange("p a n -> p (a n)")
        emb_parts = sb("emb_parts", [P, EMB_CHUNKS, 2 * BATCHES], F32R)
        film_sums = sb("film_sums", [P, 2 * CHUNKS, BATCHES])

        psum_t = ctx.enter_context(nc.psum_tensor("psum_t", [P, 2, CHUNKS, P], F32))
        psum_w = ctx.enter_context(nc.psum_tensor("psum_w", [P, 2, DIM], F32))
        psum_k = ctx.enter_context(nc.psum_tensor("psum_k", [P, TILES, DIM], F32))
        quads = psum_k[:, :, :].rearrange("p a (b n) -> p (a b) n", n=GROUP)
        att_psum = quads[:, 0:CHUNKS, :]
        att_turned_psum = psum_k[:, 0, :].rearrange("p (g n) -> p g n", n=P)
        film_rows_psum = psum_t[0:2 * BATCHES, 1, :, :].rearrange("p c n -> p (c n)")
        film_psum = psum_t[:, 1, :, :].rearrange("p a (c b) -> p (a c) b", b=2 * BATCHES)[:, 0:2 * CHUNKS, :]
        condition_psum = psum_w[:, 1, P:P + EMB_CHUNKS * BATCHES].rearrange("p (c b) -> p c b", b=BATCHES)

        def y_psum_of(t):
            at = CHUNKS * (t % 2)
            return quads[:, at:at + CHUNKS, :]

        params_loaded = [sem("params_loaded_0"), sem("params_loaded_1")]
        params_turned, params_ready = sem("params_turned"), sem("params_ready")
        masks_loaded, consts_step, masks_step = sem("masks_loaded"), sem("consts_step"), sem("masks_step")
        emb_loaded, emb_silu, emb_turned, emb_parts_ready = (
            sem("emb_loaded"), sem("emb_silu"), sem("emb_turned"), sem("emb_parts_ready"))
        film_high_ready, film_low_ready, film_used, film_copied, film_turned, film_step = (
            sem("film_high_ready"), sem("film_low_ready"), sem("film_used"), sem("film_copied"),
            sem("film_turned"), sem("film_step"))
        raw_loaded = [sem("raw_loaded_0"), sem("raw_loaded_1")]
        mask_rows_loaded, mask_top_step = [sem("mask_rows_loaded_0"), sem("mask_rows_loaded_1")], sem("mask_top_step")
        bias_q_loaded, bias_v_loaded, bias_v_ready, bias_o_loaded = (
            sem("bias_q_loaded"), sem("bias_v_loaded"), sem("bias_v_ready"), sem("bias_o_loaded"))
        w_high_ready, w_low_ready = sem("w_high_ready"), sem("w_low_ready")
        x_tile_loaded = [sem(f"x_tile_loaded_{t}") for t in range(TILES)]
        x_loaded, x_stats_done, x_moments_done, x_scale_done, xn_ready = (
            sem("x_loaded"), sem("x_stats_done"), sem("x_moments_done"), sem("x_scale_done"), sem("xn_ready"))
        xT_psum, xT_ready, xT_high_ready, xT_low_ready = (
            sem("xT_psum"), sem("xT_ready"), sem("xT_high_ready"), sem("xT_low_ready"))
        k_psum, k_max_done, k_max_turned, k_top_step, k_shift_ready = (
            sem("k_psum"), sem("k_max_done"), sem("k_max_turned"), sem("k_top_step"), sem("k_shift_ready"))
        k_shift_spread, k_shift_rows_ready, k_shifted, k_exp_ready = (
            sem("k_shift_spread"), sem("k_shift_rows_ready"), sem("k_shifted"), sem("k_exp_ready"))
        v_psum, v_ready, v_masks_ready = sem("v_psum"), sem("v_ready"), sem("v_masks_ready")
        q_psum, q_biased, q_max_done, q_shifted, q_exp_ready = (
            sem("q_psum"), sem("q_biased"), sem("q_max_done"), sem("q_shifted"), sem("q_exp_ready"))
        att_done, att_step, att_built, att_turned, att_ready = (
            sem("att_done"), sem("att_step"), sem("att_built"), sem("att_turned"), sem("att_ready"))
        qT_psum, qT_ready = sem("qT_psum"), sem("qT_ready")
        y_psum, q_rsum_done, y_ready, y_stats_done, y_moments_done, y_scale_done, yn_ready = (
            sem("y_psum"), sem("q_rsum_done"), sem("y_ready"), sem("y_stats_done"),
            sem("y_moments_done"), sem("y_scale_done"), sem("yn_ready"))
        yT_psum, gate_ready, g_high_ready, g_low_ready = (
            sem("yT_psum"), sem("gate_ready"), sem("g_high_ready"), sem("g_low_ready"))
        o_psum, res_loaded, res_biased, o_added, stored = (
            sem("o_psum"), sem("res_loaded"), sem("res_biased"), sem("o_added"), sem("stored"))
        last_res_loaded, last_stored = sem("last_res_loaded"), sem("last_stored")
        table_loaded = sem("table_loaded")
        minus_half_ready, head_blocks_ready = sem("minus_half_ready"), sem("head_blocks_ready")
        waits_passed = sem("waits_passed")

        MASK_STEPS = 6
        HEAD_BLOCK_PIECES = sum(2 + 2 * (h // CHUNKS) for h in HEADS)
        ATT_STEPS = 3 + CHUNKS
        FILM_STEPS = 6

        block = ctx.enter_context(nc.Block())

        def film_slot(layer, part):
            n = RAW_PARTS.index(("film", layer, part))
            return raw[:, n % 2 * CHUNKS:(n % 2 + 1) * CHUNKS, :], raw_loaded[n % 2], 16 * (n // 2 + 1)

        mask_rows = [m[:, :, :] for m in (y, x_res)]

        def wait_apart(eng, semaphore, value):
            eng.wait_ge(semaphore, value)
            eng.sem_inc(waits_passed, 1)

        def run_iterations(eng, iteration, output_stage):
            for layer in range(LAYERS):
                first, last = layer * BATCHES, layer * BATCHES + BATCHES - 1
                iteration(layer, first, first > 0, True)
                with eng.Fori(first + 1, last) as i:
                    iteration(layer, i, True, True)
                iteration(layer, last, True, last + 1 < ITERS)
            output_stage(LAYERS - 1, ITERS - 1)

        def fixed(i, value):
            return isinstance(i, int) and i == value

        def residual_of(j):
            return x_in if fixed(j, ITERS - 1) else x_res

        def gated_of(j):
            return (xT_high, xT_low) if fixed(j, ITERS - 1) else (gT_high, gT_low)

        LAST_0, FIRST_1 = BATCHES - 1, BATCHES

        @block.sync
        def _(sp):
            def key(layer, name):
                return a[("L0_cond_", "L1_cond_")[layer] + name]

            def load_raw(n):
                kind, layer, part = RAW_PARTS[n]
                if n >= 2:
                    kind_before = RAW_PARTS[n - 2][0]
                    used = sum(p[0] == kind_before for p in RAW_PARTS[:n - 1])
                    if kind_before == "film":
                        sp.wait_ge(film_low_ready, CHUNKS * used)
                    else:
                        sp.wait_ge(w_low_ready, CHUNKS * used)
                slot = raw[:, n % 2 * CHUNKS:(n % 2 + 1) * CHUNKS, :]
                if kind == "film":
                    weights = key(layer, ("film_emb_W", "W_emb")[layer])[
                        part % 2 * EMB // 2:(part % 2 + 1) * EMB // 2, part // 2 * DIM:(part // 2 + 1) * DIM]
                else:
                    weights = key(layer, NAMES[layer][part])
                sp.dma_start(slot, weights.rearrange("(c p) n -> p c n", p=P)).then_inc(raw_loaded[n % 2], 16)

            def load_x(i, layer):
                if layer:
                    sp.wait_ge(stored, 16 * (i - BATCHES + 1))
                sp.dma_start(x_in[:, :, :], rows(source[layer], i - BATCHES * layer)).then_inc(x_loaded, 16)

            def load_bias(layer, m, to, loaded):
                sp.dma_start(to, key(layer, BIAS_NAMES[layer][m]).partition_broadcast(P)).then_inc(loaded, 16)

            def load_params(layer):
                at = 0
                for name in PARAM_NAMES[layer]:
                    n = a[name].shape[0] // P
                    sp.dma_start(param_in[at:at + n, layer, :], a[name].rearrange("(c p) -> c p", p=P))\
                      .then_inc(params_loaded[layer], 16)
                    at += n

            bias_v_row = bias_v[:, :, :].rearrange("p g n -> p (g n)")
            for t in range(TILES):
                sp.dma_start(x_in[:, t, :], rows(source[0], 0)[:, t, :]).then_inc(x_tile_loaded[t], 16)
            load_raw(0)
            load_params(0)
            sp.dma_start(emb, a["cond_2048"]).then_inc(emb_loaded, 16)
            load_params(1)
            sp.dma_start(masked_in[:, :, :], a["mask_BxS_ik0"].rearrange("b (p t) -> p b t", t=TILES))\
              .then_inc(masks_loaded, 16)
            sp.dma_start(v_mask[:, BATCHES:ITERS, :],
                         a["mask_BxSx1_fk1"].rearrange("b (p t) o -> p b (t o)", t=TILES)).then_inc(masks_loaded, 16)
            load_raw(1)
            load_bias(0, Q, bias_q[:, :], bias_q_loaded)
            load_bias(0, V, bias_v_row, bias_v_loaded)
            load_bias(0, O, bias_o[:, :], bias_o_loaded)
            load_raw(2)
            half = BATCHES // 2
            for n in range(2):
                sp.dma_start(mask_rows[n], a["mask_BxSx1_fk1"][n * half:(n + 1) * half, :, 0].partition_broadcast(P))\
                  .then_inc(mask_rows_loaded[n], 16)

            def iteration(layer, i, with_output, with_next):
                if fixed(i, FIRST_1):
                    load_raw(RAW_IN_LAST_0)
                if with_next:
                    sp.wait_ge(xT_psum, CHUNKS * (i + 1))
                    load_x(i + 1, 1 if fixed(i, LAST_0) else layer)
                else:
                    sp.wait_ge(xT_psum, CHUNKS * ITERS)
                    sp.dma_start(x_in[:, :, :], rows(source[layer], i - BATCHES * layer)).then_inc(last_res_loaded, 16)
                if fixed(i, 0):
                    for n in range(RAW_BEFORE_0, RAW_IN_0):
                        load_raw(n)
                if with_output:
                    sp.wait_ge(mask_top_step, 2)
                    load_residual(0 if fixed(i, FIRST_1) else layer, i - 1)
                if fixed(i, LAST_0):
                    for n in range(RAW_IN_0, RAW_IN_LAST_0):
                        load_raw(n)
                    sp.wait_ge(q_biased, TILES * BATCHES)
                    load_bias(1, Q, bias_q[:, :], bias_q_loaded)
                    sp.wait_ge(att_built, BATCHES)
                    load_bias(1, V, bias_v_row, bias_v_loaded)
                if with_output:
                    store(0 if fixed(i, FIRST_1) else layer, i - 1)
                if fixed(i, FIRST_1):
                    sp.wait_ge(res_biased, TILES * BATCHES)
                    load_bias(1, O, bias_o[:, :], bias_o_loaded)

            def load_residual(layer, j):
                sp.dma_start(x_res[:, :, :], rows(source[layer], j - BATCHES * layer)).then_inc(res_loaded, 16)

            def store(layer, j):
                sp.wait_ge(o_added, TILES * (j + 1))
                sp.dma_start(rows(target[layer], j - BATCHES * layer), x_res[:, :, :]).then_inc(stored, 16)
                wait_apart(sp, stored, 16 * (j + 1))

            def output_stage(layer, j):
                for t in range(TILES):
                    sp.wait_ge(o_added, TILES * j + t + 1)
                    sp.dma_start(rows(target[layer], j - BATCHES * layer)[:, t, :], residual_of(j)[:, t, :])\
                      .then_inc(last_stored, 16)

            run_iterations(sp, iteration, output_stage)
            sp.wait_ge(stored, 16 * (ITERS - 1))
            sp.wait_ge(last_stored, 16 * TILES)

        @block.tensor
        def _(pe):
            def split_products(tiles, high, low, w, done, before=None):
                for c in range(CHUNKS):
                    if before is not None:
                        before(c)
                    for t, bank in tiles:
                        rows_of_tile = slice(t * P, (t + 1) * P)
                        for n, (lhs, rhs) in enumerate(((high, w_high), (high, w_low), (low, w_high))):
                            mm = pe.matmul(bank, lhs[:, c, rows_of_tile], rhs[w][:, c, :],
                                           start=(c == 0 and n == 0), stop=(c == CHUNKS - 1 and n == 2))
                        if c == CHUNKS - 1:
                            mm.then_inc(done, 1)

            def project(tiles, m, done, before=None):
                split_products(tiles, xT_high, xT_low, m, done, before)

            def weights_split(layer, n):
                pe.wait_ge(w_high_ready, CHUNKS * (4 * layer + n + 1))
                pe.wait_ge(w_low_ready, CHUNKS * (4 * layer + n + 1))

            def film_part(layer, part):
                if part == 0:
                    if layer:
                        pe.wait_ge(gate_ready, CHUNKS * LAST_0)
                    else:
                        pe.wait_ge(xT_ready, CHUNKS)
                    pe.wait_ge(emb_parts_ready, 2)
                if part == 2:
                    pe.wait_ge(film_copied, 2 * layer + 1)
                for c in range(CHUNKS):
                    pe.wait_ge(film_low_ready, CHUNKS * (FILM_PARTS * layer + part) + c + 1)
                    for weights in (w_high, w_low):
                        first, last = part % 2 == c == 0 and weights is w_high, part % 2 and c == CHUNKS - 1
                        mm = pe.matmul(film_rows_psum, emb_parts[:, part % 2 * CHUNKS + c, :],
                                       weights[FILM_AT[layer]][:, c, :], start=first,
                                       stop=bool(last and weights is w_low))
                    mm.then_inc(film_used, 1)

            def turn_film(layer):
                pe.wait_ge(film_copied, 2 * layer + 2)
                for c in range(2 * CHUNKS):
                    mm = pe.transpose(film_psum[:, c, :], film_rows[:, c * P:(c + 1) * P],
                                      ident[0:2 * BATCHES, 0:2 * BATCHES])
                mm.then_inc(film_turned, 1)

            def turn_x(i, c):
                if c == 0:
                    pe.wait_ge(xn_ready, TILES * (i + 1))
                if c >= 2:
                    pe.wait_ge(xT_ready, CHUNKS * i + c - 1)
                elif not fixed(i, 0):
                    pe.wait_ge(qT_ready, TILES * (i - 1) + c + 3)
                for t in range(TILES):
                    mm = pe.transpose(psum_t[:, c % 2, t, :], x_in[:, t, c * P:(c + 1) * P], ident[:, :])
                mm.then_inc(xT_psum, 1)

            def turn_y(j, c):
                if c == 0:
                    pe.wait_ge(yn_ready, TILES * (j + 1))
                if c < 2:
                    pe.wait_ge(xT_ready, CHUNKS * (min(j + 2, ITERS) if isinstance(j, int) else j + 2) - 1 + c)
                else:
                    pe.wait_ge(gate_ready, CHUNKS * j + c - 1)
                for t in range(TILES):
                    mm = pe.transpose(psum_t[:, c % 2, t, :], y[:, t, c * P:(c + 1) * P], ident[:, :])
                mm.then_inc(yT_psum, 1)

            def out_projection(layer, j, *tiles):
                def gate_split(c):
                    pe.wait_ge(g_low_ready, CHUNKS * j + c + 1)

                if 0 in tiles:
                    weights_split(layer, 3)
                if tiles[-1] >= 2 or fixed(j, ITERS - 1):
                    pe.wait_ge(o_added, TILES * j + tiles[-1] - 1)
                else:
                    pe.wait_ge(q_biased, TILES * (j + 1) + tiles[-1] + 3)
                split_products([(t, psum_w[:, t % 2, :]) for t in tiles], *gated_of(j), O, o_psum,
                               gate_split if 0 in tiles else None)

            def output_stage(layer, j):
                turn_y(j, 2)
                turn_y(j, 3)
                out_projection(layer, j, 0, 1)
                out_projection(layer, j, 2)
                out_projection(layer, j, 3)

            def turn_params(layer):
                pe.wait_ge(params_loaded[layer], 16 * len(PARAM_NAMES[layer]))
                pe.transpose(psum_w[:, layer, 0:PARAMS], param_in[:, layer, :], ident[0:PARAMS, 0:PARAMS])\
                  .then_inc(params_turned, 1)

            def turn_condition():
                pe.wait_ge(emb_silu, 1)
                for c in range(EMB_CHUNKS):
                    mm = pe.transpose(condition_psum[:, c, :],
                                      emb[:, c * P:(c + 1) * P], ident[0:BATCHES, 0:BATCHES])
                mm.then_inc(emb_turned, 1)

            pe.wait_ge(consts_step, 3)
            turn_params(0)
            for c in range(CHUNKS):
                turn_x(0, c)

            def iteration(layer, i, with_output, with_next):
                with_film, layer_film = fixed(i, 0) or fixed(i, LAST_0), int(fixed(i, LAST_0))

                def k_ready(c):
                    if fixed(i, 0):
                        pe.wait_ge(w_low_ready, c + 1)
                    pe.wait_ge(xT_low_ready, CHUNKS * i + c + 1)

                if fixed(i, FIRST_1):
                    weights_split(1, 0)
                if fixed(i, 0):
                    project([(t, psum_k[:, t, :]) for t in range(TILES)], K, k_psum, k_ready)
                else:
                    for t in range(TILES):
                        if t == 0:
                            pe.wait_ge(y_ready, TILES * (i - 1) + 3)
                        if t == 2:
                            pe.wait_ge(y_ready, TILES * i)
                        if with_output and t == 3:
                            turn_y(i - 1, 0)
                            turn_y(i - 1, 1)
                        project([(t, psum_k[:, t, :])], K, k_psum, k_ready if t == 0 else None)

                def v_projection(t):
                    if t >= 2:
                        pe.wait_ge(v_ready, TILES * i + t - 1)
                    elif t == 1 and fixed(i, 0):
                        pe.wait_ge(emb_parts_ready, 2)
                    project([(t, psum_w[:, t % 2, :])], V, v_psum)

                if fixed(i, layer * BATCHES):
                    weights_split(layer, 1)
                if fixed(i, 0):
                    turn_params(1)
                    turn_condition()
                    pe.wait_ge(params_ready, 1)
                if with_output:
                    turn_y(i - 1, 2)
                    turn_y(i - 1, 3)
                v_projection(0)
                v_projection(1)
                pe.wait_ge(k_max_done, TILES * (i + 1))
                if with_output:
                    pe.wait_ge(gate_ready, CHUNKS * (i - 1) + 3)
                else:
                    pe.wait_ge(xT_ready, CHUNKS * i + 3)
                for c in range(CHUNKS):
                    mm = pe.transpose(psum_t[:, 0, c, :], k_max[:, c * P:(c + 1) * P], ident[:, :])
                mm.then_inc(k_max_turned, 1)
                v_projection(2)
                pe.wait_ge(k_shift_ready, i + 1)
                pe.matmul(psum_t[:, 0, :, :].rearrange("p c n -> p (c n)"), ones[:, :],
                          k_shift[:, :, :].rearrange("p c n -> p (c n)"), start=True, stop=True)\
                  .then_inc(k_shift_spread, 1)
                v_projection(3)
                if fixed(i, layer * BATCHES):
                    weights_split(layer, 2)
                for t in range(TILES):
                    if t < 2:
                        pe.wait_ge(v_ready, TILES * i + t + 3)
                    else:
                        pe.wait_ge(q_biased, TILES * i + t - 1)
                    project([(t, psum_w[:, t % 2, :])], Q, q_psum)
                    if with_film and t % 2 == 0:
                        film_part(layer_film, t // 2)
                pe.wait_ge(k_exp_ready, TILES * (i + 1))
                pe.wait_ge(v_ready, TILES * (i + 1))
                pe.wait_ge(v_masks_ready, 2 * (i + 1))
                for g in range(CHUNKS):
                    for t in range(TILES):
                        mm = pe.matmul(att_psum[:, g, 0:VCOLS], k_exp[:, t, g * P:(g + 1) * P], v[:, t, g, :],
                                       start=(t == 0), stop=(t == TILES - 1))
                mm.then_inc(att_done, 1)
                if with_film:
                    film_part(layer_film, 2)

                def turn_att():
                    pe.wait_ge(att_built, i + 1)
                    for g in range(CHUNKS):
                        mm = pe.transpose(att_turned_psum[:, g, :], att_of[layer][:, g, 0:P], ident[:, :])
                    mm.then_inc(att_turned, 1)

                def turn_q(t):
                    pe.wait_ge(q_exp_ready, TILES * i + t + 1)
                    if t == 0:
                        pe.wait_ge(k_shift_rows_ready, i + 1)
                    elif t == 1:
                        if with_film:
                            pe.wait_ge(film_step, FILM_STEPS * layer_film + 1)
                        elif with_output:
                            pe.wait_ge(gate_ready, CHUNKS * i)
                        else:
                            pe.wait_ge(xT_ready, CHUNKS * i + 4)
                    else:
                        pe.wait_ge(qT_ready, TILES * i + t - 1)
                    for c in range(CHUNKS):
                        mm = pe.transpose(psum_t[:, t % 2, c, :], q[:, t, c * P:(c + 1) * P], ident[:, :])
                    mm.then_inc(qT_psum, 1)

                def attend(t):
                    pe.wait_ge(qT_ready, TILES * i + t + 1)
                    if t == 0:
                        pe.wait_ge(att_ready, i + 1)
                    if t >= 2:
                        pe.wait_ge(y_ready, TILES * i + t - 1)
                    for g in range(CHUNKS):
                        mm = pe.matmul(y_psum_of(t)[:, g, 0:BCOLS], qT[:, t, g, :], att_of[layer][:, g, :],
                                       start=True, stop=True)
                    mm.then_inc(y_psum, 1)

                out_layer = 0 if fixed(i, FIRST_1) else layer
                if with_output:
                    out_projection(out_layer, i - 1, 0)
                if with_film:
                    film_part(layer_film, 3)
                if with_output and with_next:
                    out_projection(out_layer, i - 1, 1)
                if with_film:
                    turn_film(layer_film)
                if layer == 0:
                    turn_att()
                turn_q(0)
                turn_q(1)
                if with_output and with_next:
                    out_projection(out_layer, i - 1, 2)
                turn_q(2)
                turn_q(3)
                if with_next and not with_output:
                    turn_x(i + 1, 0)
                    turn_x(i + 1, 1)
                attend(0)
                attend(1)
                if with_next:
                    if with_output:
                        turn_x(i + 1, 0)
                        turn_x(i + 1, 1)
                        out_projection(out_layer, i - 1, 3)
                    turn_x(i + 1, 2)
                attend(2)
                if with_next:
                    turn_x(i + 1, 3)
                attend(3)
                if not with_next:
                    out_projection(out_layer, i - 1, 1)
                    out_projection(out_layer, i - 1, 2)
                    turn_y(i, 0)
                    turn_y(i, 1)
                    out_projection(out_layer, i - 1, 3)

            run_iterations(pe, iteration, output_stage)

        @block.vector
        def _(dve):
            m0, m1 = slice(0, BATCHES), slice(BATCHES, ITERS)

            def next_x(i):
                if not fixed(i, 0):
                    dve.wait_ge(x_loaded, 16 * i)
                for t in range(TILES):
                    if fixed(i, 0):
                        dve.wait_ge(x_tile_loaded[t], 16)
                    dve.bn_stats(x_stats[:, t, :], x_in[:, t, :]).then_inc(x_stats_done, 1)
                for t in range(TILES):
                    wait_apart(dve, x_stats_done, TILES * i + t + 1)
                    dve.bn_aggr(x_moments[:, t, :], x_stats[:, t, :]).then_inc(x_moments_done, 1)

            def next_xn(i):
                dve.wait_ge(x_scale_done, 2 * (i + 1))
                dve.wait_ge(x_moments_done, TILES * (i + 1))
                for t in range(TILES):
                    dve.tensor_scalar(x_in[:, t, :], x_in[:, t, :], x_moments[:, t, 0:1], x_rstd[:, t:t + 1],
                                      ALU.subtract, ALU.mult).then_inc(xn_ready, 1)

            def split_weight(layer, n, c):
                m = SPLIT_ORDER[n]
                slot = RAW_PARTS.index(("weights", layer, m)) % 2
                dve.wait_ge(w_high_ready, CHUNKS * (4 * layer + n) + c + 1)
                dve.tensor_tensor(w_low[m][:, c, :], raw[:, slot * CHUNKS + c, :], w_high[m][:, c, :], ALU.subtract)\
                   .then_inc(w_low_ready, 1)

            def split_weights(layer, n):
                for c in range(CHUNKS):
                    split_weight(layer, n, c)

            def split_first_x(c):
                dve.wait_ge(xT_high_ready, c + 1)
                dve.tensor_tensor(xT_low[:, c, :], xT[:, c % 2, :], xT_high[:, c, :], ALU.subtract)\
                   .then_inc(xT_low_ready, 1)

            def v_bias_blocks(layer):
                dve.wait_ge(bias_v_loaded, 16 * (layer + 1))
                dve.wait_ge(head_blocks_ready, HEAD_BLOCK_PIECES)
                dve.tensor_tensor(bias_v[:, :, :], bias_v[:, :, :],
                                  head_blocks[layer][:, :].unsqueeze(1).to_broadcast([P, CHUNKS, P]), ALU.mult)\
                   .then_inc(bias_v_ready, 1)

            def copy_params(layer):
                dve.wait_ge(params_turned, layer + 1)
                dve.tensor_copy(params[:, layer, :], psum_w[:, layer, 0:PARAMS]).then_inc(params_ready, 1)

            def greatest_masks(n):
                half = BATCHES // 2
                dve.wait_ge(mask_rows_loaded[n], 16)
                dve.tensor_reduce(mask_top[:, n * half:(n + 1) * half], mask_rows[n], AX_X, ALU.max)\
                   .then_inc(mask_top_step, 1)

            def relative_mask():
                dve.wait_ge(mask_top_step, 2)
                dve.tensor_scalar(mask_top[:, :], mask_top[:, :], -1.0, 1.0, ALU.mult, ALU.add)\
                   .then_inc(mask_top_step, 1)
                dve.wait_ge(mask_top_step, 3)
                dve.tensor_scalar(mask_top[:, :], mask_top[:, :], MASKED_1, None, ALU.mult).then_inc(mask_top_step, 1)
                dve.wait_ge(mask_top_step, 4)
                dve.tensor_tensor(k_mask[:, m1, :], k_mask[:, m1, :],
                                  mask_top[:, :].unsqueeze(2).to_broadcast([P, BATCHES, TILES]), ALU.subtract)\
                   .then_inc(mask_top_step, 1)

            dve.memset(table_scratch[:, :], 0.0).then_inc(table_loaded, 1)
            dve.memset(minus_half[:, :], -0.5).then_inc(minus_half_ready, 1)
            next_x(0)
            next_xn(0)
            copy_params(0)
            split_weight(0, 0, 0)
            for c in range(1, CHUNKS):
                split_weight(0, 0, c)
                split_first_x(c - 1)
            split_first_x(CHUNKS - 1)
            dve.wait_ge(masks_loaded, 32)
            dve.memset(sum_mask[:, m1, :], 1.0).then_inc(masks_step, 1)
            dve.tensor_scalar(k_mask[:, m0, :], masked_in[:, :, :], 1.0, MASKED_0,
                              ALU.is_equal, ALU.mult).then_inc(masks_step, 1)
            dve.tensor_scalar(v_mask[:, m0, :], masked_in[:, :, :], 1.0, None, ALU.not_equal).then_inc(masks_step, 1)
            dve.tensor_scalar(sum_mask[:, m0, :], masked_in[:, :, :], 1.0, None, ALU.not_equal).then_inc(masks_step, 1)
            dve.tensor_scalar(k_mask[:, m1, :], v_mask[:, m1, :], -1.0, 1.0, ALU.mult, ALU.add).then_inc(masks_step, 1)
            dve.wait_ge(masks_step, 5)
            dve.tensor_scalar(k_mask[:, m1, :], k_mask[:, m1, :], MASKED_1, None, ALU.mult).then_inc(masks_step, 1)
            dve.wait_ge(masks_step, MASK_STEPS)
            split_weights(0, 1)

            def split_film(layer, part):
                slot = film_slot(layer, part)[0]
                high, low = w_high[FILM_AT[layer]], w_low[FILM_AT[layer]]
                for c in range(CHUNKS):
                    dve.wait_ge(film_high_ready, CHUNKS * (FILM_PARTS * layer + part) + c + 1)
                    dve.tensor_tensor(low[:, c, :], slot[:, c, :], high[:, c, :], ALU.subtract)\
                       .then_inc(film_low_ready, 1)

            def copy_film_rows(layer, half):
                dve.wait_ge(film_used, CHUNKS * (FILM_PARTS * layer + 2 * half + 2))
                dve.tensor_copy(film_rows[:, half * DIM:(half + 1) * DIM], film_rows_psum).then_inc(film_copied, 1)

            def film(layer):
                at = slice(layer * BATCHES, (layer + 1) * BATCHES)
                scale = film_scale[:, at, :].rearrange("p b c -> p c b")
                shift = film_shift[:, at, :].rearrange("p b c -> p c b")

                def param(r):
                    return params[:, layer, r:r + CHUNKS].unsqueeze(2).to_broadcast([P, CHUNKS, BATCHES])

                steps = FILM_STEPS * layer
                dve.wait_ge(film_turned, layer + 1)
                dve.tensor_reduce(film_sums[:, :, :], film_psum.rearrange("p c (h b) -> p c b h", h=2), AX_X, ALU.add)\
                   .then_inc(film_step, 1)
                dve.wait_ge(film_step, steps + 1)
                dve.tensor_tensor(scale, film_sums[:, 0:CHUNKS, :], param(FILM_EMB_BIAS), ALU.add).then_inc(film_step, 1)
                dve.wait_ge(film_step, steps + 2)
                dve.scalar_tensor_tensor(out=shift, in0=scale, scalar=1.0, in1=param(FILM_BIAS),
                                         op0=ALU.add, op1=ALU.mult).then_inc(film_step, 1)
                dve.wait_ge(film_step, steps + 3)
                dve.scalar_tensor_tensor(out=scale, in0=scale, scalar=1.0, in1=param(FILM_SCALE),
                                         op0=ALU.add, op1=ALU.mult).then_inc(film_step, 1)
                dve.tensor_tensor(shift, shift, film_sums[:, CHUNKS:2 * CHUNKS, :], ALU.add).then_inc(film_step, 1)
                dve.wait_ge(film_step, steps + 5)
                dve.tensor_tensor(shift, shift, param(FILM_EMB_BIAS + CHUNKS), ALU.add).then_inc(film_step, 1)

            def normalise_y(j):
                dve.wait_ge(y_scale_done, 2 * (j + 1))
                dve.wait_ge(y_moments_done, TILES * (j + 1))
                for t in range(TILES):
                    dve.tensor_scalar(y[:, t, :], y[:, t, :], y_moments[:, t, 0:1], y_rstd[:, t:t + 1],
                                      ALU.subtract, ALU.mult).then_inc(yn_ready, 1)

            def split_gate(j, c):
                dve.wait_ge(g_high_ready, CHUNKS * j + c + 1)
                high, low = gated_of(j)
                dve.tensor_tensor(low[:, c, :], gate[:, c % 2, :], high[:, c, :], ALU.subtract)\
                   .then_inc(g_low_ready, 1)

            def add_residual(j, t):
                dve.wait_ge(o_psum, TILES * j + t + 1)
                dve.wait_ge(res_biased, TILES * j + t + 1)
                x_sum = residual_of(j)[:, t, :]
                dve.tensor_tensor(x_sum, x_sum, psum_w[:, t % 2, :], ALU.add).then_inc(o_added, 1)

            def output_stage(layer, j):
                split_gate(j, 2)
                split_gate(j, 3)
                for t in range(TILES):
                    add_residual(j, t)

            def iteration(layer, i, with_output, with_next):
                with_film, layer_film = fixed(i, 0) or fixed(i, LAST_0), int(fixed(i, LAST_0))
                heads = HEADS[layer]
                per_group = heads // CHUNKS
                width = DIM // heads
                att = att_of[layer]
                if with_output:
                    normalise_y(i - 1)
                for t in range(TILES):
                    if t == TILES - 1 and fixed(i, layer * BATCHES):
                        split_weights(layer, 2)
                    dve.wait_ge(k_psum, TILES * i + t + 1)
                    mask = k_mask[:, bass.ds(i, 1), t:t + 1].rearrange("p a t -> p (a t)")
                    if t == 0:
                        dve.tensor_scalar(k_max[:, :], psum_k[:, t, :], mask, None, ALU.add).then_inc(k_max_done, 1)
                    else:
                        dve.wait_ge(k_max_done, TILES * i + t)
                        dve.scalar_tensor_tensor(out=k_max[:, :], in0=psum_k[:, t, :], scalar=mask,
                                                 in1=k_max[:, :], op0=ALU.add, op1=ALU.max).then_inc(k_max_done, 1)
                if fixed(i, 0):
                    dve.wait_ge(emb_turned, 1)
                    copy_params(1)
                    dve.tensor_copy(emb_parts[:, :, 0:BATCHES], condition_psum).then_inc(emb_parts_ready, 1)
                    dve.wait_ge(emb_parts_ready, 1)
                    dve.tensor_tensor(emb_parts[:, :, BATCHES:2 * BATCHES], condition_psum, emb_parts[:, :, 0:BATCHES],
                                      ALU.subtract).then_inc(emb_parts_ready, 1)
                if with_output:
                    for c in range(CHUNKS):
                        split_gate(i - 1, c)
                if fixed(i, 0):
                    greatest_masks(0)
                dve.wait_ge(k_max_turned, i + 1)
                dve.tensor_reduce(k_top[:, 0, :], psum_t[:, 0, :, :], AX_X, ALU.max).then_inc(k_top_step, 1)
                dve.wait_ge(k_top_step, 3 * i + 1)
                bias_k = params[:, layer, BK:BK + CHUNKS]
                dve.tensor_tensor(k_top[:, 1, :], k_top[:, 0, :], bias_k, ALU.add).then_inc(k_top_step, 1)
                dve.wait_ge(k_top_step, 3 * i + 2)
                dve.tensor_tensor(k_top[:, 2, :], bias_k, k_top[:, 1, :], ALU.subtract).then_inc(k_top_step, 1)
                dve.wait_ge(k_top_step, 3 * i + 3)
                dve.tensor_tensor(k_shift[:, :, :], ident[:, :].unsqueeze(1).to_broadcast([P, CHUNKS, P]),
                                  k_top[:, 2, :].unsqueeze(2).to_broadcast([P, CHUNKS, P]), ALU.mult)\
                   .then_inc(k_shift_ready, 1)
                dve.wait_ge(k_shift_rows_ready, i + 1)
                for t in range(TILES):
                    dve.tensor_tensor(k_exp[:, t, :], psum_k[:, t, :], k_shift_rows[:, :], ALU.add)\
                       .then_inc(k_shifted, 1)
                if with_film:
                    split_film(layer_film, 0)
                if fixed(i, layer * BATCHES):
                    v_bias_blocks(layer)
                    dve.wait_ge(bias_q_loaded, 16 * (layer + 1))
                if with_next:
                    next_x(i + 1)
                for t in range(TILES):
                    dve.wait_ge(q_psum, TILES * i + t + 1)
                    dve.tensor_tensor(q[:, t, :], psum_w[:, t % 2, :], bias_q[:, :], ALU.add)\
                       .then_inc(q_biased, 1)
                    dve.wait_ge(q_biased, TILES * i + t + 1)
                    dve.tensor_reduce(q_max[:, t, 0:heads], q[:, t, :].rearrange("p (h e) -> p h e", e=width),
                                      AX_X, ALU.max).then_inc(q_max_done, 1)
                    if with_film and t == 0:
                        split_film(layer_film, 1)
                if with_film:
                    copy_film_rows(layer_film, 0)
                    split_film(layer_film, 2)
                if with_next:
                    next_xn(i + 1)
                if fixed(i, 0):
                    split_film(0, 3)
                dve.wait_ge(att_done, i + 1)
                dve.tensor_copy(att_sums[:, :, :], att_psum[:, :, P:VCOLS]).then_inc(att_step, 1)
                dve.wait_ge(att_step, ATT_STEPS * i + 1)
                dve.reciprocal(att_scale[:, 0, :], att_sums[:, :, 0]).then_inc(att_step, 1)
                dve.wait_ge(att_step, ATT_STEPS * i + 2)
                dve.tensor_tensor(att_scale[:, 1, :], att_scale[:, 0, :], att_sums[:, :, 1], ALU.mult)\
                   .then_inc(att_step, 1)
                for g in range(CHUNKS):
                    dve.scalar_tensor_tensor(out=att[:, g, 0:P], in0=att_psum[:, g, 0:P],
                                             scalar=att_scale[:, 0, g:g + 1], in1=head_blocks[layer][:, :],
                                             op0=ALU.mult, op1=ALU.mult).then_inc(att_step, 1)
                dve.wait_ge(att_step, ATT_STEPS * (i + 1))
                for g in range(CHUNKS):
                    mm = dve.scalar_tensor_tensor(out=att[:, g, 0:P], in0=bias_v[:, g, :],
                                                  scalar=att_scale[:, 1, g:g + 1], in1=att[:, g, 0:P],
                                                  op0=ALU.mult, op1=ALU.add)
                mm.then_inc(att_ready if layer else att_built, 1)
                if fixed(i, LAST_0):
                    split_film(1, 3)
                if with_output:
                    add_residual(i - 1, 0)
                if with_film:
                    copy_film_rows(layer_film, 1)
                if with_output and with_next:
                    add_residual(i - 1, 1)
                if with_film:
                    film(layer_film)
                if layer == 0:
                    dve.wait_ge(att_turned, i + 1)
                    dve.tensor_copy(att[:, :, 0:P], att_turned_psum).then_inc(att_ready, 1)
                if fixed(i, 0):
                    greatest_masks(1)
                if fixed(i, LAST_0):
                    split_weights(1, 0)
                if with_output and with_next:
                    add_residual(i - 1, 2)
                for t in range(TILES):
                    if t == 2 and with_output and with_next:
                        add_residual(i - 1, 3)
                    ps = y_psum_of(t)
                    rsum = q_rsum[:, t, 0:heads].rearrange("p (g h) -> p g h", g=CHUNKS)
                    dve.wait_ge(y_psum, TILES * i + t + 1)
                    dve.reciprocal(rsum, ps[:, :, P:P + per_group]).then_inc(q_rsum_done, 1)
                    dve.wait_ge(q_rsum_done, TILES * i + t + 1)
                    dve.tensor_tensor(
                        y[:, t, :].rearrange("p (g h e) -> p g h e", g=CHUNKS, h=per_group),
                        ps[:, :, 0:P].rearrange("p g (h e) -> p g h e", h=per_group),
                        rsum.unsqueeze(3).to_broadcast([P, CHUNKS, per_group, width]), ALU.mult).then_inc(y_ready, 1)
                    for s in range(t - 1, t + 1) if t % 2 else ():
                        dve.wait_ge(y_ready, TILES * i + s + 1)
                        dve.bn_stats(y_stats[:, s, :], y[:, s, :]).then_inc(y_stats_done, 1)
                for t in range(TILES):
                    wait_apart(dve, y_stats_done, TILES * i + t + 1)
                    dve.bn_aggr(y_moments[:, t, :], y_stats[:, t, :]).then_inc(y_moments_done, 1)
                if not with_next:
                    add_residual(i - 1, 1)
                    normalise_y(i)
                    add_residual(i - 1, 2)
                    split_gate(i, 0)
                    split_gate(i, 1)
                    add_residual(i - 1, 3)
                if fixed(i, 0):
                    split_weights(0, 3)
                    relative_mask()
                if fixed(i, LAST_0):
                    split_weights(1, 1)
                if fixed(i, FIRST_1):
                    split_weights(1, 3)

            run_iterations(dve, iteration, output_stage)

        @block.scalar
        def _(act):
            def split_weights(layer, n):
                m = SPLIT_ORDER[n]
                at = RAW_PARTS.index(("weights", layer, m))
                act.wait_ge(raw_loaded[at % 2], 16 * (at // 2 + 1))
                if m == FILM_AT[layer]:
                    act.wait_ge(film_used, CHUNKS * FILM_PARTS * (layer + 1))
                if layer:
                    act.wait_ge({K: k_psum, V: v_psum, Q: q_psum, O: o_psum}[m], TILES * BATCHES)
                for c in range(CHUNKS):
                    act.copy(w_high[m][:, c, :], raw[:, at % 2 * CHUNKS + c, :]).then_inc(w_high_ready, 1)

            def split_film(layer, part):
                slot, loaded, count = film_slot(layer, part)
                act.wait_ge(loaded, count)
                before = CHUNKS * (FILM_PARTS * layer + part - 1)
                for c in range(CHUNKS):
                    if before >= 0:
                        act.wait_ge(film_used, before + c + 1)
                    act.copy(w_high[FILM_AT[layer]][:, c, :], slot[:, c, :]).then_inc(film_high_ready, 1)

            def scale_x(i, layer):
                for c in range(CHUNKS):
                    act.wait_ge(xT_psum, CHUNKS * i + c + 1)
                    if c >= 2:
                        act.wait_ge(xT_low_ready, CHUNKS * i + c - 1)
                    act.activation(xT[:, c % 2, :], psum_t[:, c % 2, :, :].rearrange("p t s -> p (t s)"),
                                   ACT.Identity, scale=params[:, layer, LN_SCALE + c:LN_SCALE + c + 1],
                                   bias=params[:, layer, LN_BIAS + c:LN_BIAS + c + 1]).then_inc(xT_ready, 1)
                    act.wait_ge(xT_ready, CHUNKS * i + c + 1)
                    act.copy(xT_high[:, c, :], xT[:, c % 2, :]).then_inc(xT_high_ready, 1)

            def preload_silu():
                act.activation(table_scratch[:, 1:2], table_scratch[:, 0:1], ACT.Silu).then_inc(table_loaded, 1)

            act.wait_ge(table_loaded, 1)
            preload_silu()
            split_weights(0, 0)
            act.wait_ge(params_ready, 1)
            scale_x(0, 0)
            act.wait_ge(emb_loaded, 16)
            act.activation(emb, emb, ACT.Silu).then_inc(emb_silu, 1)
            split_weights(0, 1)
            split_weights(0, 2)

            def activate(j, c):
                act.wait_ge(yT_psum, CHUNKS * j + c + 1)
                if c >= 2:
                    act.wait_ge(g_low_ready, CHUNKS * j + c - 1)
                cond = bass.ds(j, 1)
                act.activation(gate[:, c % 2, :], psum_t[:, c % 2, :, :].rearrange("p t s -> p (t s)"), ACT.Silu,
                               scale=film_scale[:, cond, c:c + 1].rearrange("p a c -> p (a c)"),
                               bias=film_shift[:, cond, c:c + 1].rearrange("p a c -> p (a c)")).then_inc(gate_ready, 1)
                act.wait_ge(gate_ready, CHUNKS * j + c + 1)
                act.copy(gated_of(j)[0][:, c, :], gate[:, c % 2, :]).then_inc(g_high_ready, 1)

            def output_stage(layer, j):
                for c in range(CHUNKS):
                    activate(j, c)

            def iteration(layer, i, with_output, with_next):
                with_film, layer_film = fixed(i, 0) or fixed(i, LAST_0), int(fixed(i, LAST_0))
                if with_output:
                    for c in range(CHUNKS):
                        activate(i - 1, c)

                def mask_v(t):
                    act.wait_ge(v_psum, TILES * i + t + 1)
                    act.activation(v[:, t, :, 0:P], psum_w[:, t % 2, :].rearrange("p (g n) -> p g n", g=CHUNKS),
                                   ACT.Copy, scale=v_mask[:, bass.ds(i, 1), t:t + 1].rearrange("p a t -> p (a t)"))\
                       .then_inc(v_ready, 1)

                if fixed(i, 0):
                    act.wait_ge(masks_step, MASK_STEPS)
                mask_v(0)
                if with_film:
                    split_film(layer_film, 0)
                mask_v(1)
                mask_v(2)
                act.wait_ge(k_shift_spread, i + 1)
                act.copy(k_shift_rows[:, :], psum_t[:, 0, :, :].rearrange("p c n -> p (c n)"))\
                   .then_inc(k_shift_rows_ready, 1)
                mask_v(3)
                for t in range(TILES):
                    act.wait_ge(k_shifted, TILES * i + t + 1)
                    act.activation(k_exp[:, t, :], k_exp[:, t, :], ACT.Exp,
                                   bias=k_mask[:, bass.ds(i, 1), t:t + 1].rearrange("p a t -> p (a t)"))\
                       .then_inc(k_exp_ready, 1)
                if with_film:
                    split_film(layer_film, 1)
                for t in range(TILES):
                    act.wait_ge(q_shifted, TILES * i + t + 1)
                    act.activation(q[:, t, :], q[:, t, :], ACT.Exp).then_inc(q_exp_ready, 1)
                    if with_film and t == 2:
                        split_film(layer_film, 2)
                if with_film:
                    split_film(layer_film, 3)
                for t in range(TILES):
                    act.wait_ge(qT_psum, TILES * i + t + 1)
                    act.copy(qT[:, t, :, :], psum_t[:, t % 2, :, :]).then_inc(qT_ready, 1)
                    if fixed(i, LAST_0) and t == 1:
                        split_weights(1, 0)
                if with_next:
                    scale_x(i + 1, 1 if fixed(i, LAST_0) else layer)
                act.wait_ge(table_loaded, i + 2)
                preload_silu()
                if fixed(i, 0):
                    split_weights(0, 3)
                if fixed(i, LAST_0):
                    split_weights(1, 1)
                    split_weights(1, 2)
                if fixed(i, FIRST_1):
                    split_weights(1, 3)

            run_iterations(act, iteration, output_stage)

        @block.gpsimd
        def _(pool):
            def scale_of(moments, var, rstd, count, done, i):
                wait_apart(pool, count, TILES * (i + 1))
                pool.tensor_scalar(var[:, :], moments[:, :, 1], EPS, None, ALU.add).then_inc(done, 1)
                pool.wait_ge(done, 2 * i + 1)
                pool.tensor_tensor(rstd[:, :], var[:, :], minus_half[:, :], ALU.pow).then_inc(done, 1)

            def split_x(i):
                for c in range(CHUNKS):
                    pool.wait_ge(xT_high_ready, CHUNKS * i + c + 1)
                    pool.tensor_tensor(xT_low[:, c, :], xT[:, c % 2, :], xT_high[:, c, :], ALU.subtract)\
                        .then_inc(xT_low_ready, 1)

            pool.memset(ident[:, :], 0.0).then_inc(consts_step, 1)
            pool.memset(ones[:, :].bitcast(F32), 1.0).then_inc(consts_step, 1)
            pool.wait_ge(consts_step, 2)
            pool.affine_select(out=ident[:, :], in_=ident[:, :], compare_op=ALU.not_equal, fill=1.0,
                               base=0, pattern=[[-1, P]], channel_multiplier=1).then_inc(consts_step, 1)
            pool.wait_ge(minus_half_ready, 1)
            scale_of(x_moments, x_var, x_rstd, x_moments_done, x_scale_done, 0)
            pieces = 0
            for layer in range(LAYERS):
                width = DIM // HEADS[layer]
                steps = [(head_blocks[layer][:, :], 0.0), (att_of[layer][:, :, :], 0.0)]
                for h in range(P // width):
                    at = slice(h * width, (h + 1) * width)
                    steps += [(att_of[layer][at, :, P + h:P + h + 1], 1.0), (head_blocks[layer][at, at], 1.0)]
                for piece, value in steps:
                    pool.memset(piece, value).then_inc(head_blocks_ready, 1)
                    pieces += 1
                    pool.wait_ge(head_blocks_ready, pieces)
            pool.wait_ge(masks_step, MASK_STEPS)
            pool.wait_ge(bias_o_loaded, 16)

            def bias_residual(j):
                if fixed(j, ITERS - 1):
                    pool.wait_ge(last_res_loaded, 16)
                else:
                    pool.wait_ge(res_loaded, 16 * (j + 1))
                for t in range(TILES):
                    x_biased = residual_of(j)[:, t, :]
                    pool.tensor_tensor(x_biased, x_biased, bias_o[:, :], ALU.add)\
                        .then_inc(res_biased, 1)

            def output_stage(layer, j):
                bias_residual(j)

            def iteration(layer, i, with_output, with_next):
                width = DIM // HEADS[layer]
                if not fixed(i, 0):
                    pool.wait_ge(att_done, i)
                for n, table in enumerate((sum_mask, v_mask)):
                    row = table[:, bass.ds(i, 1), :].rearrange("p a t -> p (a t)")
                    pool.tensor_copy(v[:, :, :, P + n], row.unsqueeze(2).to_broadcast([P, TILES, CHUNKS]))\
                        .then_inc(v_masks_ready, 1)
                if with_next:
                    scale_of(x_moments, x_var, x_rstd, x_moments_done, x_scale_done, i + 1)
                if with_output:
                    bias_residual(i - 1)
                for t in range(TILES):
                    pool.wait_ge(q_max_done, TILES * i + t + 1)
                    rows_q = q[:, t, :].rearrange("p (h e) -> p h e", e=width)
                    pool.tensor_tensor(rows_q, rows_q, q_max[:, t, 0:HEADS[layer]].unsqueeze(2)
                                       .to_broadcast([P, HEADS[layer], width]), ALU.subtract).then_inc(q_shifted, 1)
                if with_next:
                    split_x(i + 1)
                scale_of(y_moments, y_var, y_rstd, y_moments_done, y_scale_done, i)
                if fixed(i, FIRST_1):
                    pool.wait_ge(bias_o_loaded, 32)

            run_iterations(pool, iteration, output_stage)


NAMES = ({Q: "Wq", K: "Wk", V: "Wv", O: "film_out_W"}, {Q: "Wq", K: "Wk", V: "Wv", O: "W_out"})
BIAS_NAMES = ({Q: "bq", K: "bk", V: "bv", O: "film_out_b"}, {Q: "bq", K: "bk", V: "bv", O: "b_out"})
PARAM_NAMES = (
    ("L0_cond_norm_scale", "L0_cond_norm_bias", "L0_cond_bk", "L0_cond_film_norm_scale", "L0_cond_film_norm_bias",
     "L0_cond_film_emb_b"),
    ("L1_cond_ln_w", "L1_cond_ln_b", "L1_cond_bk", "L1_cond_ln2_w", "L1_cond_ln2_b", "L1_cond_b_emb"),
)


def kernel(**inputs):
    import numpy as np
    import concourse.bacc as bacc
    from concourse.bass_utils import run_bass_kernel_spmd

    nc = bacc.Bacc("TRN2", target_bir_lowering=False, num_devices=1)
    arrays, aps = {}, {}
    for name, value in inputs.items():
        value = np.ascontiguousarray(value)
        arrays[f"in_{name}"] = value
        aps[name] = nc.dram_tensor(f"in_{name}", value.shape, mybir.dt.from_np(value.dtype),
                                   kind="ExternalInput").ap()
    out = nc.dram_tensor("out_x", (BATCHES, SEQ, DIM), F32, kind="ExternalOutput").ap()
    build_program(nc, aps, out)
    result = run_bass_kernel_spmd(nc, [arrays], core_ids=[0])
    return result.results[0]["out_x"]
```
